# Optimizing a Trainium2 kernel written in Bass

```python
import numpy as np
import jax
import jax.numpy as jnp

def _softmax(x, axis=-1):
    return jax.nn.softmax(x, axis=axis)

def _gelu(x):
    return jax.nn.gelu(x, approximate=True)

def _silu(x):
    return jax.nn.silu(x)

def _sigmoid(x):
    return jax.nn.sigmoid(x)

def _layernorm(x, axis=-1, eps=1e-05):
    m = jnp.mean(x, axis=axis, keepdims=True)
    v = jnp.var(x, axis=axis, keepdims=True)
    return (x - m) / jnp.sqrt(v + eps)

def _scatter_add(tgt, idx, src, axis=0):
    return tgt.at[idx].add(src)

def _segment_sum(src, seg, n):
    return jax.ops.segment_sum(src, seg, n)
kernel_name = 'mk_sandwich_d1_jaxref_r2_930f97'

def setup_inputs(seed: int=0):
    np.random.seed(seed)
    _w = jnp.asarray

    def _L0_attn_setup():
        import jax, jax.numpy as jnp
        import numpy as np
        B, N, D, H = (8, 2048, 512, 16)
        HD = D // H
        EPS = 1e-05
        key = jax.random.key(seed)
        ks = jax.random.split(key, 18)
        s = 1.0 / np.sqrt(D)

        def lin(k):
            return (jax.random.normal(k, (D, D), jnp.float32) * s, jnp.zeros((D,), jnp.float32))
        Wg_w, Wg_b = lin(ks[0])
        Wr_w, Wr_b = lin(ks[1])
        Wk_w, Wk_b = lin(ks[2])
        Wv_w, Wv_b = lin(ks[3])
        Wo_w, Wo_b = lin(ks[4])
        mg = jax.random.uniform(ks[5], (D,), jnp.float32)
        mr = jax.random.uniform(ks[6], (D,), jnp.float32)
        mk = jax.random.uniform(ks[7], (D,), jnp.float32)
        mv = jax.random.uniform(ks[8], (D,), jnp.float32)
        w = jax.random.normal(ks[9], (H, HD), jnp.float32)
        u = jax.random.normal(ks[10], (H, HD), jnp.float32)
        x = jax.random.normal(ks[11], (B, N, D), jnp.float32)
        return {'x': x, 'Wg_w': Wg_w, 'Wg_b': Wg_b, 'Wr_w': Wr_w, 'Wr_b': Wr_b, 'Wk_w': Wk_w, 'Wk_b': Wk_b, 'Wv_w': Wv_w, 'Wv_b': Wv_b, 'Wo_w': Wo_w, 'Wo_b': Wo_b, 'mg': mg, 'mr': mr, 'mk': mk, 'mv': mv, 'w': w, 'u': u}
    _L0_attn_in = _L0_attn_setup()

    def _L0_ffn_setup():
        import jax, jax.numpy as jnp
        import numpy as np
        D_MODEL = 512
        NUM_TILES = 64
        TPC = 8
        NUM_CLUSTERS = NUM_TILES // TPC
        GRID = 16
        COMP_H = 128
        NUM_KNOTS = 8
        EPS_LN = 1e-05

        def _calibrate(scores, knots, temperature):
            K = knots.shape[0]
            normalized = jax.nn.sigmoid(scores / (temperature[0] + 1e-06))
            idx_float = normalized * (K - 1)
            idx_low = jnp.clip(idx_float.astype(jnp.int32), 0, K - 2)
            idx_high = idx_low + 1
            t = idx_float - idx_low.astype(scores.dtype)
            val_low = knots[idx_low]
            val_high = knots[idx_high]
            return val_low + t * (val_high - val_low)

        def _forward(x, signatures_raw, knot_values, temperature, compress_w1, compress_b1, compress_w2, compress_b2, spline_w1, spline_b1, spline_w2, spline_b2, directions, norm_gamma, norm_beta, output_scale):
            B, T, D = x.shape
            xf = x.reshape(-1, D)
            q = jnp.where(signatures_raw > 0.3, 1.0, jnp.where(signatures_raw < -0.3, -1.0, 0.0)).astype(signatures_raw.dtype)
            sigs = signatures_raw + jax.lax.stop_gradient(q - signatures_raw)
            cluster_sigs = jnp.sign(sigs.reshape(NUM_CLUSTERS, TPC, D).mean(axis=1))
            cluster_scores = xf @ cluster_sigs.T
            cluster_gates = _calibrate(cluster_scores, knot_values, temperature)
            cluster_idx = jnp.argmax(cluster_gates, axis=-1)
            tile_scores = xf @ sigs.T
            tile_gates = _calibrate(tile_scores, knot_values, temperature)
            gates_by_cluster = tile_gates.reshape(-1, NUM_CLUSTERS, TPC)
            sel_gates = jnp.take_along_axis(gates_by_cluster, cluster_idx[:, None, None], axis=1)[:, 0, :]
            local_idx = jnp.argmax(sel_gates, axis=-1)
            tile_idx = cluster_idx * TPC + local_idx
            h = jax.nn.gelu(xf @ compress_w1 + compress_b1, approximate=False)
            comp = jnp.tanh(h @ compress_w2 + compress_b2)
            w1 = spline_w1[tile_idx]
            b1 = spline_b1[tile_idx]
            hh = jax.nn.relu(jnp.einsum('ni,nig->ng', comp, w1) + b1)
            w2 = spline_w2[tile_idx]
            b2 = spline_b2[tile_idx]
            mag = jnp.einsum('ng,ngo->no', hh, w2) + b2
            ffn_out = mag * directions[tile_idx] * output_scale[0]
            y = xf + ffn_out
            mu = y.mean(axis=-1, keepdims=True)
            var = ((y - mu) ** 2).mean(axis=-1, keepdims=True)
            y = (y - mu) / jnp.sqrt(var + EPS_LN) * norm_gamma + norm_beta
            return y.reshape(B, T, D)
        key = jax.random.key(seed)
        ks = jax.random.split(key, 12)
        B, T = (4, 2048)
        x = jax.random.normal(ks[0], (B, T, D_MODEL), dtype=jnp.float32)
        signatures_raw = jax.random.normal(ks[1], (NUM_TILES, D_MODEL), dtype=jnp.float32) * 0.5
        knot_values = jax.nn.sigmoid(jnp.linspace(-3.0, 3.0, NUM_KNOTS).astype(jnp.float32))
        temperature = jnp.ones((1,), dtype=jnp.float32)
        compress_w1 = jax.random.normal(ks[2], (D_MODEL, COMP_H), dtype=jnp.float32) * (1.0 / np.sqrt(D_MODEL))
        compress_b1 = jnp.zeros((COMP_H,), dtype=jnp.float32)
        compress_w2 = jax.random.normal(ks[3], (COMP_H, 2), dtype=jnp.float32) * (1.0 / np.sqrt(COMP_H))
        compress_b2 = jnp.zeros((2,), dtype=jnp.float32)
        spline_w1 = jax.random.normal(ks[4], (NUM_TILES, 2, GRID), dtype=jnp.float32) * (1.0 / np.sqrt(2.0))
        spline_b1 = jnp.zeros((NUM_TILES, GRID), dtype=jnp.float32)
        spline_w2 = jax.random.normal(ks[5], (NUM_TILES, GRID, 1), dtype=jnp.float32) * (1.0 / np.sqrt(GRID))
        spline_b2 = jnp.zeros((NUM_TILES, 1), dtype=jnp.float32)
        directions = jax.random.normal(ks[6], (NUM_TILES, D_MODEL), dtype=jnp.float32) * 0.02
        norm_gamma = jnp.ones((D_MODEL,), dtype=jnp.float32)
        norm_beta = jnp.zeros((D_MODEL,), dtype=jnp.float32)
        output_scale = jnp.ones((1,), dtype=jnp.float32) * 0.1
        return dict(x=x, signatures_raw=signatures_raw, knot_values=knot_values, temperature=temperature, compress_w1=compress_w1, compress_b1=compress_b1, compress_w2=compress_w2, compress_b2=compress_b2, spline_w1=spline_w1, spline_b1=spline_b1, spline_w2=spline_w2, spline_b2=spline_b2, directions=directions, norm_gamma=norm_gamma, norm_beta=norm_beta, output_scale=output_scale)
    _L0_ffn_in = _L0_ffn_setup()
    _d = {'L0_attn_x': _L0_attn_in['x'], 'L0_attn_Wg_w': _L0_attn_in['Wg_w'], 'L0_attn_Wg_b': _L0_attn_in['Wg_b'], 'L0_attn_Wr_w': _L0_attn_in['Wr_w'], 'L0_attn_Wr_b': _L0_attn_in['Wr_b'], 'L0_attn_Wk_w': _L0_attn_in['Wk_w'], 'L0_attn_Wk_b': _L0_attn_in['Wk_b'], 'L0_attn_Wv_w': _L0_attn_in['Wv_w'], 'L0_attn_Wv_b': _L0_attn_in['Wv_b'], 'L0_attn_Wo_w': _L0_attn_in['Wo_w'], 'L0_attn_Wo_b': _L0_attn_in['Wo_b'], 'L0_attn_mg': _L0_attn_in['mg'], 'L0_attn_mr': _L0_attn_in['mr'], 'L0_attn_mk': _L0_attn_in['mk'], 'L0_attn_mv': _L0_attn_in['mv'], 'L0_attn_w': _L0_attn_in['w'], 'L0_attn_u': _L0_attn_in['u'], 'L0_ffn_signatures_raw': _L0_ffn_in['signatures_raw'], 'L0_ffn_knot_values': _L0_ffn_in['knot_values'], 'L0_ffn_temperature': _L0_ffn_in['temperature'], 'L0_ffn_compress_w1': _L0_ffn_in['compress_w1'], 'L0_ffn_compress_b1': _L0_ffn_in['compress_b1'], 'L0_ffn_compress_w2': _L0_ffn_in['compress_w2'], 'L0_ffn_compress_b2': _L0_ffn_in['compress_b2'], 'L0_ffn_spline_w1': _L0_ffn_in['spline_w1'], 'L0_ffn_spline_b1': _L0_ffn_in['spline_b1'], 'L0_ffn_spline_w2': _L0_ffn_in['spline_w2'], 'L0_ffn_spline_b2': _L0_ffn_in['spline_b2'], 'L0_ffn_directions': _L0_ffn_in['directions'], 'L0_ffn_norm_gamma': _L0_ffn_in['norm_gamma'], 'L0_ffn_norm_beta': _L0_ffn_in['norm_beta'], 'L0_ffn_output_scale': _L0_ffn_in['output_scale']}
    _x0 = _d['L0_attn_x']
    _d['L0_attn_x'] = jax.random.normal(jax.random.fold_in(jax.random.key(seed), 1), (2, 8192, 512), dtype=_x0.dtype)
    del _x0
    return _d

def reference(L0_attn_x, L0_attn_Wg_w, L0_attn_Wg_b, L0_attn_Wr_w, L0_attn_Wr_b, L0_attn_Wk_w, L0_attn_Wk_b, L0_attn_Wv_w, L0_attn_Wv_b, L0_attn_Wo_w, L0_attn_Wo_b, L0_attn_mg, L0_attn_mr, L0_attn_mk, L0_attn_mv, L0_attn_w, L0_attn_u, L0_ffn_signatures_raw, L0_ffn_knot_values, L0_ffn_temperature, L0_ffn_compress_w1, L0_ffn_compress_b1, L0_ffn_compress_w2, L0_ffn_compress_b2, L0_ffn_spline_w1, L0_ffn_spline_b1, L0_ffn_spline_w2, L0_ffn_spline_b2, L0_ffn_directions, L0_ffn_norm_gamma, L0_ffn_norm_beta, L0_ffn_output_scale):

    def _L0_attn_ref(x, Wg_w, Wg_b, Wr_w, Wr_b, Wk_w, Wk_b, Wv_w, Wv_b, Wo_w, Wo_b, mg, mr, mk, mv, w, u):
        import jax, jax.numpy as jnp
        import numpy as np
        B, N, D, H = (8, 2048, 512, 16)
        HD = D // H
        EPS = 1e-05
        b, n, d = x.shape
        x_shift = jnp.roll(x, shift=1, axis=1)

        def mix(m, W, bias):
            return (m * x + (1.0 - m) * x_shift) @ W.T + bias
        g = mix(mg, Wg_w, Wg_b).reshape(b, n, H, HD)
        r = mix(mr, Wr_w, Wr_b).reshape(b, n, H, HD)
        k = mix(mk, Wk_w, Wk_b).reshape(b, n, H, HD)
        v = mix(mv, Wv_w, Wv_b).reshape(b, n, H, HD)
        kv = k * v
        decay = jnp.exp(-jnp.exp(w))
        kv_t = jnp.swapaxes(kv, 0, 1)

        def step(acc, kvt):
            acc = decay * acc + kvt
            return (acc, acc)
        _, accs = jax.lax.scan(step, jnp.zeros((b, H, HD), x.dtype), kv_t)
        wkv = jnp.swapaxes(accs, 0, 1) + u * kv
        rw = r * wkv
        mean = jnp.mean(rw, axis=-1, keepdims=True)
        var = jnp.var(rw, axis=-1, keepdims=True)
        ln = (rw - mean) * jax.lax.rsqrt(var + EPS)
        out = (jax.nn.sigmoid(g) * ln).reshape(b, n, d)
        return out @ Wo_w.T + Wo_b

    def _L0_ffn_ref(x, signatures_raw, knot_values, temperature, compress_w1, compress_b1, compress_w2, compress_b2, spline_w1, spline_b1, spline_w2, spline_b2, directions, norm_gamma, norm_beta, output_scale):
        import jax, jax.numpy as jnp
        import numpy as np
        D_MODEL = 512
        NUM_TILES = 64
        TPC = 8
        NUM_CLUSTERS = NUM_TILES // TPC
        GRID = 16
        COMP_H = 128
        NUM_KNOTS = 8
        EPS_LN = 1e-05

        def _calibrate(scores, knots, temperature):
            K = knots.shape[0]
            normalized = jax.nn.sigmoid(scores / (temperature[0] + 1e-06))
            idx_float = normalized * (K - 1)
            idx_low = jnp.clip(idx_float.astype(jnp.int32), 0, K - 2)
            idx_high = idx_low + 1
            t = idx_float - idx_low.astype(scores.dtype)
            val_low = knots[idx_low]
            val_high = knots[idx_high]
            return val_low + t * (val_high - val_low)

        def _forward(x, signatures_raw, knot_values, temperature, compress_w1, compress_b1, compress_w2, compress_b2, spline_w1, spline_b1, spline_w2, spline_b2, directions, norm_gamma, norm_beta, output_scale):
            B, T, D = x.shape
            xf = x.reshape(-1, D)
            q = jnp.where(signatures_raw > 0.3, 1.0, jnp.where(signatures_raw < -0.3, -1.0, 0.0)).astype(signatures_raw.dtype)
            sigs = signatures_raw + jax.lax.stop_gradient(q - signatures_raw)
            cluster_sigs = jnp.sign(sigs.reshape(NUM_CLUSTERS, TPC, D).mean(axis=1))
            cluster_scores = xf @ cluster_sigs.T
            cluster_gates = _calibrate(cluster_scores, knot_values, temperature)
            cluster_idx = jnp.argmax(cluster_gates, axis=-1)
            tile_scores = xf @ sigs.T
            tile_gates = _calibrate(tile_scores, knot_values, temperature)
            gates_by_cluster = tile_gates.reshape(-1, NUM_CLUSTERS, TPC)
            sel_gates = jnp.take_along_axis(gates_by_cluster, cluster_idx[:, None, None], axis=1)[:, 0, :]
            local_idx = jnp.argmax(sel_gates, axis=-1)
            tile_idx = cluster_idx * TPC + local_idx
            h = jax.nn.gelu(xf @ compress_w1 + compress_b1, approximate=False)
            comp = jnp.tanh(h @ compress_w2 + compress_b2)
            w1 = spline_w1[tile_idx]
            b1 = spline_b1[tile_idx]
            hh = jax.nn.relu(jnp.einsum('ni,nig->ng', comp, w1) + b1)
            w2 = spline_w2[tile_idx]
            b2 = spline_b2[tile_idx]
            mag = jnp.einsum('ng,ngo->no', hh, w2) + b2
            ffn_out = mag * directions[tile_idx] * output_scale[0]
            y = xf + ffn_out
            mu = y.mean(axis=-1, keepdims=True)
            var = ((y - mu) ** 2).mean(axis=-1, keepdims=True)
            y = (y - mu) / jnp.sqrt(var + EPS_LN) * norm_gamma + norm_beta
            return y.reshape(B, T, D)
        return _forward(x, signatures_raw, knot_values, temperature, compress_w1, compress_b1, compress_w2, compress_b2, spline_w1, spline_b1, spline_w2, spline_b2, directions, norm_gamma, norm_beta, output_scale)
    x = L0_attn_x
    x = x + _layernorm(_L0_attn_ref(_layernorm(x, axis=-1), L0_attn_Wg_w, L0_attn_Wg_b, L0_attn_Wr_w, L0_attn_Wr_b, L0_attn_Wk_w, L0_attn_Wk_b, L0_attn_Wv_w, L0_attn_Wv_b, L0_attn_Wo_w, L0_attn_Wo_b, L0_attn_mg, L0_attn_mr, L0_attn_mk, L0_attn_mv, L0_attn_w, L0_attn_u), axis=-1)
    x = x + _layernorm(_L0_ffn_ref(_layernorm(x, axis=-1), L0_ffn_signatures_raw, L0_ffn_knot_values, L0_ffn_temperature, L0_ffn_compress_w1, L0_ffn_compress_b1, L0_ffn_compress_w2, L0_ffn_compress_b2, L0_ffn_spline_w1, L0_ffn_spline_b1, L0_ffn_spline_w2, L0_ffn_spline_b2, L0_ffn_directions, L0_ffn_norm_gamma, L0_ffn_norm_beta, L0_ffn_output_scale), axis=-1)
    return x

_drawn_inputs = setup_inputs


def setup_inputs(seed=0):
    import zlib

    import numpy as np

    out = dict(_drawn_inputs(seed))
    spreads = {'L0_attn_Wg_b': (0.0, 0.271),
     'L0_attn_Wr_b': (0.0, 0.1),
     'L0_attn_Wk_b': (0.0, 0.1),
     'L0_attn_Wv_b': (0.0, 0.1),
     'L0_attn_Wo_b': (0.0, 0.1),
     'L0_ffn_compress_b1': (0.0, 0.8),
     'L0_ffn_compress_b2': (0.0, 2.0),
     'L0_ffn_spline_b1': (0.0, 2.0),
     'L0_ffn_spline_b2': (0.0, 2.0),
     'L0_ffn_norm_gamma': (1.0, 0.2),
     'L0_ffn_norm_beta': (0.0, 0.1)}
    factors = {'L0_ffn_signatures_raw': 8.0,
     'L0_ffn_knot_values': 8.0,
     'L0_ffn_compress_w1': 8.0,
     'L0_ffn_compress_w2': 8.0,
     'L0_ffn_spline_w1': 8.0,
     'L0_ffn_spline_w2': 8.0,
     'L0_ffn_directions': 8.0}
    for name, (base, spread) in spreads.items():
        noise = np.random.default_rng([zlib.crc32(name.encode()), seed]).standard_normal(out[name].shape)
        drawn = base * np.exp(spread * noise) if base else spread * noise
        out[name] = jnp.asarray(drawn.astype(out[name].dtype))
    for name, factor in factors.items():
        out[name] = (out[name] * factor).astype(out[name].dtype)
    return out
```

```python
from contextlib import ExitStack
from typing import NamedTuple

import numpy as np

import concourse.bass as bass
from concourse import mybir

P = 128
B, N, D = 2, 8192, 512
H = 16
HD = D // H
C = D // P
G = 2
T = G * P
BLOCKS = N // T
STEPS = B * BLOCKS
TILES, CLUSTERS = 64, 8
TPC = TILES // CLUSTERS
GRID = 16
HID = 128
KNOTS = 8
SEGS = KNOTS - 1
COLS = TILES + CLUSTERS
TABLE = 4 * GRID + 1
EPS = 1e-5
EXP_MAX = 88.5

F32 = mybir.dt.float32
ALU = mybir.AluOpType
ACT = mybir.ActivationFunctionType
X = mybir.AxisListType.X

V, K, R, GATE = range(4)
(VEC_MV, VEC_MK, VEC_MR, VEC_MG, VEC_BV, VEC_BK, VEC_BR, VEC_BG, VEC_W, VEC_U) = range(10)
ROW_GAMMA, ROW_BETA, ROW_KNOTS = 0, D, 2 * D
ROW_TEMP = ROW_KNOTS + KNOTS
ROW_OUTSCALE = ROW_TEMP + 1
ROWS = ROW_OUTSCALE + 1
CST_IDENT = 0
CST_CENTER = CST_IDENT + P
CST_HEADVAR = CST_CENTER + P
CST_SPREAD = CST_HEADVAR + C * H
CST_FLOOR = CST_SPREAD + C * P
CST_SEG = CST_FLOOR + KNOTS
CST_IOTA = CST_SEG + SEGS
CST_IOTA8 = CST_IOTA + CLUSTERS
CST_COLS = CST_IOTA8 + CLUSTERS

GATE_LINKS = 39
MAG_LINKS = 9


class Step(NamedTuple):
    j: object
    u: int
    least: int

    @property
    def n(self):
        return self.j * 2 + self.u

    def back(self, k):
        u = (self.u - k) % 2
        return Step(self.j + (self.u - k - u) // 2, u, self.least - k)


def shape_constants():
    c = np.zeros((P, CST_COLS), np.float32)
    p = np.arange(P)
    same_head = (p[:, None] // HD == p[None, :] // HD)
    c[:, CST_IDENT:CST_IDENT + P] = np.eye(P)
    c[:, CST_CENTER:CST_CENTER + P] = np.eye(P) - same_head / HD
    per = P // HD
    for m in range(C):
        c[p, CST_HEADVAR + m * H + m * per + p // HD] = 4.0 / HD
        c[m * per + p // HD, CST_SPREAD + m * P + p] = 1.0
    c[:, CST_FLOOR:CST_FLOOR + KNOTS] = [-1.0] + list(range(1, SEGS)) + [1e30]
    c[:, CST_SEG:CST_SEG + SEGS] = np.arange(SEGS)
    c[:, CST_IOTA:CST_IOTA + CLUSTERS] = np.arange(CLUSTERS)
    c[:, CST_IOTA8:CST_IOTA8 + CLUSTERS] = np.arange(CLUSTERS) + CLUSTERS
    return c


def build(nc, x, w_proj, w_out, sig_raw, comp_w1, comp_w2, table, directions, vecs, comp_b1,
          rows, bias_rows, consts, out):
    ctx = ExitStack()
    with ctx:
        def sb(name, shape):
            return ctx.enter_context(nc.sbuf_tensor(name, shape, F32))

        def psum(name, shape):
            return ctx.enter_context(nc.psum_tensor(name, shape, F32))

        def sem(name):
            return ctx.enter_context(nc.semaphore(name))

        wT = [sb(f"wT{q}", [P, C, D]) for q in range(4)]
        woT = sb("woT", [P, C, D])
        sigT = sb("sigT", [P, C, COLS])
        w1T = sb("w1T", [P, C, HID])
        w2 = sb("w2", [P, 2])
        tabs = sb("tabs", [P, TABLE])
        dirs = sb("dirs", [P, D])
        vec = sb("vec", [P, 10, C])
        b1 = sb("b1", [P, 1])
        row = sb("row", [P, ROWS])
        brow = sb("brow", [1, D + 2])
        cst = sb("cst", [P, CST_COLS])
        raw = sb("raw", [P, C, TILES])
        q_pos = sb("q_pos", [P, C, TILES])
        q_neg = sb("q_neg", [P, C, TILES])
        csum = sb("csum", [P, C, CLUSTERS])
        ones = sb("ones", [1, P])
        mhalf = sb("mhalf", [P, T])
        expw = sb("expw", [P, C])
        decay = sb("decay", [P, C])
        bg_half = sb("bg_half", [P, C])
        neg_it = sb("neg_it", [P, 3])
        curve = sb("curve", [P, 3, SEGS])
        seed_x = sb("seed_x", [B, D])
        seed_st = sb("seed_st", [B, 6])
        seed_mv = sb("seed_mv", [B, 2])
        seed_ve = sb("seed_ve", [B, 1])
        seed_rs = sb("seed_rs", [B, 1])
        seed_xn = sb("seed_xn", [B, D])
        seed = sb("seed", [P, C, B])

        xa = [sb(f"xa{u}", [P, G, D]) for u in range(2)]
        xn = sb("xn", [P, G, D])
        xnT = [sb(f"xnT{u}", [P, C, T + 1]) for u in range(2)]
        dx = sb("dx", [P, C, T])
        mix = [[sb(f"mix{u}_{q}", [P, C, T]) for q in range(4)] for u in range(2)]
        vS = sb("vS", [P, C, T])
        kv = sb("kv", [P, C, T])
        acc = [sb(f"acc{u}", [P, C, T]) for u in range(2)]
        rw = [sb(f"rw{u}", [P, C, T]) for u in range(2)]
        tg = [sb(f"tg{u}", [P, C, T]) for u in range(2)]
        sq = sb("sq", [P, C, T])
        head_ve = sb("head_ve", [H, T])
        head_rs = sb("head_rs", [H, T])
        oT = sb("oT", [P, C, T])
        at = sb("at", [P, G, D])
        x1 = [sb(f"x1_{u}", [P, G, D]) for u in range(2)]
        xf = [sb(f"xf{u}", [P, G, D]) for u in range(2)]
        xfT = sb("xfT", [P, C, T])
        yb = sb("yb", [P, G, D])
        st = {k: sb(f"st_{k}", [P, G, 6]) for k in "abcde"}
        mv = {k: sb(f"mv_{k}", [P, G, 2]) for k in "abcde"}
        ve = {k: sb(f"ve_{k}", [P, G]) for k in "abcde"}
        rs = {k: sb(f"rs_{k}", [P, G]) for k in "abcde"}
        sc = sb("sc", [P, G, COLS])
        hS = sb("hS", [P, T])
        ex = [sb(f"ex{i}", [P, G, CLUSTERS]) for i in range(2)]
        E = G * CLUSTERS
        sel = sb("sel", [P, G, TPC])
        den = sb("den", [P, E])
        pos = sb("pos", [P, E])
        steps_ge = sb("steps_ge", [P, KNOTS, E])
        seg = sb("seg", [P, SEGS, E])
        pick = sb("pick", [P, 3, SEGS, E])
        piece = sb("piece", [P, 3, E])
        val = sb("val", [P, G, CLUSTERS])
        best = sb("best", [P, G])
        is_best = sb("is_best", [P, G, CLUSTERS])
        cand = sb("cand", [P, G, CLUSTERS])
        first = sb("first", [P, G])
        hot = [sb(f"hot{i}", [P, G, CLUSTERS]) for i in range(2)]
        prod = sb("prod", [P, G, TPC, CLUSTERS])
        onehot = sb("onehot", [P, G, TILES])
        ohT = sb("ohT", [P, P])
        comp = sb("comp", [P, G, 2])
        tS = sb("tS", [P, G, TABLE])
        hp = sb("hp", [P, G, 2, GRID])
        hh = sb("hh", [P, G, GRID])
        mag = sb("mag", [P, G])

        proj_ps = [psum(f"proj_ps{q}", [P, 2, T]) for q in range(4)]
        turn_ps = psum("turn_ps", [P, 512])
        head_ps = [psum(f"head_ps{p}", [P, 512]) for p in range(2)]
        side_ps = psum("side_ps", [P, 512])

        weights_in = sem("weights_in")
        xa_in = [sem(f"xa_in{u}") for u in range(2)]
        xr_in = [sem(f"xr_in{u}") for u in range(2)]
        stored = [sem(f"stored{u}") for u in range(2)]
        setup_v = sem("setup_v")
        setup_a = sem("setup_a")
        setup_p = sem("setup_p")
        setup_t = sem("setup_t")
        ready = sem("ready")
        stat = {k: sem(f"stat_{k}") for k in "abcde"}
        mean_var = {k: sem(f"mean_var_{k}") for k in "abcde"}
        var_eps = {k: sem(f"var_eps_{k}") for k in "abcde"}
        rstd = {k: sem(f"rstd_{k}") for k in "abcde"}
        xn_done = sem("xn_done")
        xn_turned = sem("xn_turned")
        xnT_done = sem("xnT_done")
        dx_done = sem("dx_done")
        mixed = sem("mixed")
        proj_done = sem("proj_done")
        v_done = sem("v_done")
        kv_done = sem("kv_done")
        scan_done = sem("scan_done")
        wkv_done = sem("wkv_done")
        rw_done = sem("rw_done")
        tg_done = sem("tg_done")
        centered = sem("centered")
        sq_done = sem("sq_done")
        cg_done = sem("cg_done")
        var_done = sem("var_done")
        head_ve_done = sem("head_ve_done")
        head_rs_done = sem("head_rs_done")
        spread = sem("spread")
        oT_done = sem("oT_done")
        wo_done = sem("wo_done")
        at_done = sem("at_done")
        x1_done = sem("x1_done")
        xf_done = sem("xf_done")
        xf_turned = sem("xf_turned")
        xfT_done = sem("xfT_done")
        hidden_ps = sem("hidden_ps")
        scores_ps = sem("scores_ps")
        sc_done = sem("sc_done")
        ex_done = sem("ex_done")
        routed = sem("routed")
        hS_done = sem("hS_done")
        comp_ps = sem("comp_ps")
        comp_done = sem("comp_done")
        ohT_ps = sem("ohT_ps")
        ohT_done = sem("ohT_done")
        tables_ps = sem("tables_ps")
        spline = sem("spline")
        dirs_ps = sem("dirs_ps")
        y_done = sem("y_done")
        scaled = sem("scaled")
        z_done = sem("z_done")
        zn_done = sem("zn_done")
        fin_done = sem("fin_done")

        x_t = x.rearrange("s (j g p) d -> s j p g d", g=G, p=P)
        out_t = out.rearrange("s (j g p) d -> s j p g d", g=G, p=P)
        ident = cst[:, CST_IDENT:CST_IDENT + P]
        center = cst[:, CST_CENTER:CST_CENTER + P]
        N_WEIGHTS = 16

        def schedule(eng, body):
            body(Step(0, 0, 0), True, True, False, False)
            body(Step(0, 1, 1), True, True, True, False)
            with eng.Fori(1, BLOCKS - 1) as j:
                for u in range(2):
                    body(Step(j, u, 2 + u), True, True, True, True)
            j = BLOCKS - 1
            body(Step(j, 0, 2 * j), True, True, True, True)
            body(Step(j, 1, 2 * j + 1), False, True, True, True)
            body(Step(j + 1, 0, 2 * j + 2), False, False, True, True)
            body(Step(j + 1, 1, 2 * j + 3), False, False, False, True)

        block = ctx.enter_context(nc.Block())

        @block.sync
        def _(sp):
            for u in range(2):
                sp.dma_start(xa[u][:], x_t[u, 0]).then_inc(xa_in[u], 16)
            sp.dma_start(seed_x[:], x[:, N - 1, :]).then_inc(weights_in, 16)
            sp.dma_start(cst[:], consts).then_inc(weights_in, 16)
            sp.dma_start(vec[:], vecs).then_inc(weights_in, 16)
            for q in range(4):
                sp.dma_start(wT[q][:], w_proj[q].rearrange("(c p) o -> p c o", p=P)).then_inc(weights_in, 16)
            sp.dma_start(woT[:], w_out.rearrange("(c p) o -> p c o", p=P)).then_inc(weights_in, 16)
            sp.dma_start(raw[:], sig_raw.rearrange("(c p) o -> p c o", p=P)).then_inc(weights_in, 16)
            sp.dma_start(w1T[:], comp_w1.rearrange("(c p) o -> p c o", p=P)).then_inc(weights_in, 16)
            sp.dma_start(w2[:], comp_w2).then_inc(weights_in, 16)
            sp.dma_start(tabs[:], table).then_inc(weights_in, 16)
            sp.dma_start(dirs[:], directions).then_inc(weights_in, 16)
            sp.dma_start(b1[:], comp_b1).then_inc(weights_in, 16)
            sp.dma_start(row[:], rows).then_inc(weights_in, 16)
            sp.dma_start(brow[:], bias_rows).then_inc(weights_in, 16)

            def body(s, do_mix, do_proj, do_norm, do_route):
                h, f = s.back(1), s.back(2)
                if do_mix and s.least + 2 < STEPS and do_proj:
                    sp.wait_ge(xn_done, G * s.n + G)
                    sp.nop(nofuse=True)
                    sp.dma_start(xa[s.u][:], x_t[s.u, s.j + 1]).then_inc(xa_in[s.u], 16)
                if do_norm:
                    if h.least >= 2:
                        sp.wait_ge(stored[h.u], h.j * 16)
                        sp.nop(nofuse=True)
                    sp.dma_start(x1[h.u][:], x_t[h.u, h.j]).then_inc(xr_in[h.u], 16)
                if do_route:
                    sp.wait_ge(fin_done, G * f.n + G)
                    sp.nop(nofuse=True)
                    sp.dma_start(out_t[f.u, f.j], x1[f.u][:]).then_inc(stored[f.u], 16)

            schedule(sp, body)
            for u in range(2):
                sp.wait_ge(stored[u], 16 * BLOCKS)

        @block.gpsimd
        def _(pool):
            pool.memset(mhalf[:], -0.5).then_inc(setup_p, 1)
            pool.memset(ones[:], 1.0).then_inc(setup_p, 1)
            for u in range(2):
                pool.memset(acc[u][:], 0.0).then_inc(setup_p, 1)
            pool.wait_ge(setup_p, 4)
            pool.wait_ge(setup_v, 3)
            pool.tensor_tensor(seed_rs[:], seed_ve[:], mhalf[0:B, 0:1], ALU.pow).then_inc(setup_p, 1)

            def root(k, s):
                pool.wait_ge(var_eps[k], s.n + 1)
                pool.tensor_tensor(rs[k][:], ve[k][:], mhalf[:, 0:G], ALU.pow).then_inc(rstd[k], 1)

            def delta(s):
                pool.wait_ge(xnT_done, 3 * s.n + 3)
                if s.least >= 1:
                    pool.wait_ge(mixed, 4 * C * s.n)
                pool.tensor_tensor(dx[:], xnT[s.u][:, :, 1:T + 1], xnT[s.u][:, :, 0:T],
                                   ALU.subtract).then_inc(dx_done, 1)

            def body(s, do_mix, do_proj, do_norm, do_route):
                a, h, f = s.back(-1), s.back(1), s.back(2)
                if do_mix:
                    root("a", a)
                if do_norm:
                    pool.wait_ge(head_ve_done, h.n + 1)
                    if h.least >= 1:
                        pool.wait_ge(spread, 2 * h.n)
                    pool.tensor_tensor(head_rs[:], head_ve[:], mhalf[0:H, :], ALU.pow).then_inc(head_rs_done, 1)
                if do_mix:
                    delta(a)
                if do_norm:
                    root("b", h)
                    pool.wait_ge(xr_in[h.u], h.j * 16 + 16)
                    for g in range(G):
                        pool.wait_ge(at_done, G * h.n + g + 1)
                        pool.tensor_tensor(x1[h.u][:, g, :], x1[h.u][:, g, :], at[:, g, :],
                                           ALU.add).then_inc(x1_done, 1)
                if do_route:
                    root("d", f)
                if do_norm:
                    root("c", h)
                if do_route:
                    root("e", f)
                    for g in range(G):
                        pool.wait_ge(zn_done, G * f.n + g + 1)
                        pool.tensor_tensor(x1[f.u][:, g, :], x1[f.u][:, g, :], yb[:, g, :],
                                           ALU.add).then_inc(fin_done, 1)

            first_step = Step(0, 0, 0)
            root("a", first_step)
            delta(first_step)
            schedule(pool, body)

        @block.scalar
        def _(act):
            act.wait_ge(weights_in, 16 * N_WEIGHTS)
            act.activation(expw[:], vec[:, VEC_W, :], ACT.Exp).then_inc(setup_a, 1)
            act.wait_ge(setup_a, 1)
            act.activation(decay[:], expw[:], ACT.Exp, scale=-1.0).then_inc(setup_a, 1)
            act.wait_ge(setup_t, 1)
            act.activation(seed[:], turn_ps[:, 0:C * B].rearrange("p (c s) -> p c s", c=C),
                           ACT.Copy).then_inc(setup_a, 1)
            act.wait_ge(setup_a, 3)

            def turned_input(s):
                if s.least >= 2:
                    act.wait_ge(mixed, 4 * C * s.n - 4 * C)
                    act.wait_ge(dx_done, s.n - 1)
                before = xnT[s.u][:, :, T:T + 1] if s.least >= 2 else seed[:, :, s.u:s.u + 1]
                act.activation(xnT[s.u][:, :, 0:1], before, ACT.Copy).then_inc(xnT_done, 1)
                act.wait_ge(xnT_done, 3 * s.n + 1)
                for g, bank in enumerate((turn_ps, side_ps)):
                    act.wait_ge(xn_turned, G * s.n + g + 1)
                    act.activation(xnT[s.u][:, :, 1 + g * P:1 + g * P + P],
                                   bank[:].rearrange("p (c t) -> p c t", c=C), ACT.Copy).then_inc(xnT_done, 1)

            def values(s, p):
                act.wait_ge(proj_done, 8 * s.n + 4 * p + V + 1)
                for i in range(2):
                    m = 2 * p + i
                    if s.least >= 1:
                        act.wait_ge(kv_done, C * s.n - C + m + 1)
                    act.activation(vS[:, m, :], proj_ps[V][:, i, :], ACT.Identity,
                                   bias=vec[:, VEC_BV, m:m + 1]).then_inc(v_done, 1)

            def gates(s, p):
                act.wait_ge(proj_done, 8 * s.n + 4 * p + GATE + 1)
                if s.least >= 2:
                    act.wait_ge(oT_done, 2 * s.n - 2)
                for i in range(2):
                    m = 2 * p + i
                    act.activation(tg[s.u][:, m, :], proj_ps[GATE][:, i, :], ACT.Tanh, scale=0.5,
                                   bias=bg_half[:, m:m + 1]).then_inc(tg_done, 1)

            def body(s, do_mix, do_proj, do_norm, do_route):
                a, h, f = s.back(-1), s.back(1), s.back(2)
                if do_proj:
                    values(s, 0)
                if do_route:
                    for g, bank in enumerate((turn_ps, side_ps)):
                        act.wait_ge(xf_turned, G * f.n + g + 1)
                        if f.least >= 1:
                            act.wait_ge(scores_ps, f.n)
                        act.activation(xfT[:, :, g * P:g * P + P],
                                       bank[:].rearrange("p (c t) -> p c t", c=C), ACT.Copy).then_inc(xfT_done, 1)
                if do_norm:
                    for p in range(2):
                        act.wait_ge(centered, 2 * h.n + p + 1)
                        if h.least >= 1:
                            act.wait_ge(var_done, h.n)
                        act.activation(sq[:, 2 * p:2 * p + 2, :],
                                       head_ps[p][:].rearrange("p (m t) -> p m t", m=2),
                                       ACT.Square).then_inc(sq_done, 1)
                if do_proj:
                    gates(s, 0)
                if do_route:
                    act.wait_ge(sc_done, f.n + 1)
                    act.activation(ex[0][:], sc[:, :, TILES:COLS], ACT.Exp).then_inc(ex_done, 1)
                if do_proj:
                    values(s, 1)
                if do_route:
                    act.wait_ge(routed, GATE_LINKS * f.n + 20)
                    act.activation(ex[1][:], sel[:], ACT.Exp).then_inc(ex_done, 1)
                    act.wait_ge(hidden_ps, f.n + 1)
                    if f.least >= 1:
                        act.wait_ge(comp_ps, f.n)
                    act.activation(hS[:], side_ps[:, 0:T], ACT.Gelu, bias=b1[:, 0:1]).then_inc(hS_done, 1)
                if do_mix:
                    turned_input(a)
                if do_route:
                    act.wait_ge(comp_ps, f.n + 1)
                    if f.least >= 1:
                        act.wait_ge(spline, MAG_LINKS * f.n)
                    act.activation(comp[:], side_ps[:, 0:2 * G].rearrange("p (g o) -> p g o", g=G),
                                   ACT.Tanh).then_inc(comp_done, 1)
                    act.wait_ge(ohT_ps, f.n + 1)
                    if f.least >= 1:
                        act.wait_ge(dirs_ps, G * f.n)
                    act.activation(ohT[:], turn_ps[:, 0:P], ACT.Copy).then_inc(ohT_done, 1)
                if do_proj:
                    gates(s, 1)

            turned_input(Step(0, 0, 0))
            schedule(act, body)

        @block.tensor
        def _(pe):
            pe.wait_ge(weights_in, 16 * N_WEIGHTS)
            pe.wait_ge(setup_v, 4)
            for c in range(C):
                last = pe.transpose(turn_ps[:, c * B:c * B + B], seed_xn[:, c * P:c * P + P], ident[0:B, 0:B])
            last.then_inc(setup_t, 1)
            pe.wait_ge(setup_a, 3)

            def turn_input(s):
                for g, bank in enumerate((turn_ps, side_ps)):
                    pe.wait_ge(xn_done, G * s.n + g + 1)
                    if s.least >= 1:
                        pe.wait_ge(xnT_done, 3 * s.n)
                    for c in range(C):
                        last = pe.transpose(bank[:, c * P:c * P + P], xn[:, g, c * P:c * P + P], ident)
                    last.then_inc(xn_turned, 1)

            def project(s, p, q):
                pe.wait_ge(mixed, 4 * C * s.n + 4 * C)
                reader = {V: v_done, K: kv_done, R: rw_done, GATE: tg_done}[q]
                if p or s.least >= 1:
                    pe.wait_ge(reader, C * s.n + 2 * p)
                for i in range(2):
                    m = 2 * p + i
                    for c in range(C):
                        last = pe.matmul(proj_ps[q][:, i, :], wT[q][:, c, m * P:m * P + P], mix[s.u][q][:, c, :],
                                         start=(c == 0), stop=(c == C - 1))
                last.then_inc(proj_done, 1)

            def body(s, do_mix, do_proj, do_norm, do_route):
                a, h, f = s.back(-1), s.back(1), s.back(2)
                if do_proj:
                    project(s, 0, V)
                    project(s, 0, K)
                if do_route:
                    for g, bank in enumerate((turn_ps, side_ps)):
                        pe.wait_ge(xf_done, G * f.n + g + 1)
                        pe.wait_ge(xnT_done, (3 * s.n + 3) if do_proj else 3 * STEPS)
                        if f.least >= 1:
                            pe.wait_ge(y_done, G * f.n)
                        for c in range(C):
                            last = pe.transpose(bank[:, c * P:c * P + P], xf[f.u][:, g, c * P:c * P + P], ident)
                        last.then_inc(xf_turned, 1)
                if do_norm:
                    for p in range(2):
                        pe.wait_ge(rw_done, C * h.n + 2 * p + 2)
                        if h.least >= 1:
                            pe.wait_ge(at_done, G * h.n)
                        for i in range(2):
                            last = pe.matmul(head_ps[p][:, i * T:i * T + T], center, rw[h.u][:, 2 * p + i, :],
                                             start=True, stop=True)
                        last.then_inc(centered, 1)
                if do_proj:
                    project(s, 0, R)
                    project(s, 0, GATE)
                if do_route:
                    pe.wait_ge(xfT_done, G * f.n + G)
                    for g in range(G):
                        for c in range(C):
                            last = pe.matmul(turn_ps[:, g * COLS:g * COLS + COLS], xfT[:, c, g * P:g * P + P],
                                             sigT[:, c, :], start=(c == 0), stop=(c == C - 1))
                    last.then_inc(scores_ps, 1)
                    for c in range(C):
                        last = pe.matmul(side_ps[:, 0:T], w1T[:, c, :], xfT[:, c, :],
                                         start=(c == 0), stop=(c == C - 1))
                    last.then_inc(hidden_ps, 1)
                if do_norm:
                    pe.wait_ge(sq_done, 2 * h.n + 2)
                    pe.wait_ge(cg_done, 2 * h.n + 1)
                    for m in range(C):
                        last = pe.matmul(head_ps[0][0:H, 0:T], cst[:, CST_HEADVAR + m * H:CST_HEADVAR + m * H + H],
                                         sq[:, m, :], start=(m == 0), stop=(m == C - 1))
                    last.then_inc(var_done, 1)
                if do_proj:
                    project(s, 1, V)
                    project(s, 1, K)
                if do_mix:
                    if do_route:
                        pe.wait_ge(sc_done, f.n + 1)
                        pe.wait_ge(hS_done, f.n + 1)
                    turn_input(a)
                if do_norm:
                    pe.wait_ge(head_rs_done, h.n + 1)
                    for p in range(2):
                        pe.wait_ge(cg_done, 2 * h.n + 1 + p)
                        for i in range(2):
                            m = 2 * p + i
                            last = pe.matmul(head_ps[p][:, i * T:i * T + T],
                                             cst[0:H, CST_SPREAD + m * P:CST_SPREAD + m * P + P], head_rs[:],
                                             start=True, stop=True)
                        last.then_inc(spread, 1)
                if do_proj:
                    project(s, 1, R)
                if do_route:
                    pe.wait_ge(hS_done, f.n + 1)
                    if do_mix:
                        pe.wait_ge(xnT_done, 3 * a.n + 3)
                    for g in range(G):
                        pe.matmul(side_ps[:, 2 * g:2 * g + 2], hS[:, g * P:g * P + P], w2[:], start=True, stop=False)
                        last = pe.matmul(side_ps[:, 2 * g:2 * g + 2], ones[:], brow[:, D:D + 2],
                                         start=False, stop=True)
                    last.then_inc(comp_ps, 1)
                    pe.wait_ge(routed, GATE_LINKS * f.n + GATE_LINKS)
                    pe.transpose(turn_ps[:, 0:P], onehot[:].rearrange("p g e -> p (g e)"), ident).then_inc(ohT_ps, 1)
                if do_norm:
                    pe.wait_ge(oT_done, 2 * h.n + 2)
                    for g in range(G):
                        pe.matmul(head_ps[g][:], ones[:], brow[:, 0:D], start=True, stop=False)
                        for c in range(C):
                            last = pe.matmul(head_ps[g][:], oT[:, c, g * P:g * P + P], woT[:, c, :],
                                             start=False, stop=(c == C - 1))
                        last.then_inc(wo_done, 1)
                if do_proj:
                    project(s, 1, GATE)
                if do_route:
                    pe.wait_ge(comp_done, f.n + 1)
                    pe.wait_ge(ohT_done, f.n + 1)
                    for g, bank in enumerate((turn_ps, side_ps)):
                        of_g = slice(g * TILES, g * TILES + TILES)
                        pe.matmul(bank[:, 0:TABLE], ohT[of_g, :], tabs[of_g, :],
                                  start=True, stop=True).then_inc(tables_ps, 1)
                    for g, bank in enumerate((turn_ps, side_ps)):
                        of_g = slice(g * TILES, g * TILES + TILES)
                        pe.wait_ge(spline, MAG_LINKS * f.n + 1 + g)
                        pe.matmul(bank[:], ohT[of_g, :], dirs[of_g, :], start=True, stop=True).then_inc(dirs_ps, 1)

            turn_input(Step(0, 0, 0))
            schedule(pe, body)

        @block.vector
        def _(dve):
            dve.wait_ge(weights_in, 16 * N_WEIGHTS)
            dve.bn_stats(seed_st[:], seed_x[:]).then_inc(setup_v, 1)
            dve.wait_ge(setup_v, 1)
            dve.bn_aggr(seed_mv[:], seed_st[:]).then_inc(setup_v, 1)
            dve.wait_ge(setup_v, 2)
            dve.tensor_scalar(seed_ve[:], seed_mv[:, 1:2], EPS, None, ALU.add).then_inc(setup_v, 1)
            dve.wait_ge(setup_p, 5)
            dve.tensor_scalar(seed_xn[:], seed_x[:], seed_mv[:, 0:1], seed_rs[:], ALU.subtract,
                              ALU.mult).then_inc(setup_v, 1)
            dve.tensor_scalar(neg_it[:, 0:1], row[:, ROW_TEMP:ROW_TEMP + 1], 1e-6, None, ALU.add).then_inc(ready, 1)
            dve.wait_ge(ready, 1)
            dve.reciprocal(neg_it[:, 1:2], neg_it[:, 0:1]).then_inc(ready, 1)
            dve.wait_ge(ready, 2)
            dve.tensor_scalar(neg_it[:, 2:3], neg_it[:, 1:2], -1.0, None, ALU.mult).then_inc(ready, 1)
            dve.tensor_scalar(bg_half[:], vec[:, VEC_BG, :], 0.5, None, ALU.mult).then_inc(ready, 1)
            dve.tensor_copy(curve[:, 0, :], row[:, ROW_KNOTS:ROW_KNOTS + SEGS]).then_inc(ready, 1)
            dve.tensor_tensor(curve[:, 1, :], row[:, ROW_KNOTS + 1:ROW_KNOTS + KNOTS],
                              row[:, ROW_KNOTS:ROW_KNOTS + SEGS], ALU.subtract).then_inc(ready, 1)
            dve.tensor_copy(curve[:, 2, :], cst[:, CST_SEG:CST_SEG + SEGS]).then_inc(ready, 1)
            dve.tensor_scalar(q_pos[:], raw[:], 0.3, None, ALU.is_gt).then_inc(ready, 1)
            dve.tensor_scalar(q_neg[:], raw[:], -0.3, None, ALU.is_lt).then_inc(ready, 1)
            dve.wait_ge(ready, 9)
            dve.tensor_tensor(q_pos[:], q_pos[:], q_neg[:], ALU.subtract).then_inc(ready, 1)
            dve.wait_ge(ready, 10)
            dve.tensor_tensor(q_pos[:], q_pos[:], raw[:], ALU.subtract).then_inc(ready, 1)
            dve.wait_ge(ready, 11)
            dve.tensor_tensor(sigT[:, :, 0:TILES], raw[:], q_pos[:], ALU.add).then_inc(ready, 1)
            dve.wait_ge(ready, 12)
            for c in range(C):
                dve.tensor_reduce(csum[:, c, :], sigT[:, c, 0:TILES].rearrange("p (k t) -> p k t", k=CLUSTERS),
                                  X, ALU.add).then_inc(ready, 1)
            dve.wait_ge(ready, 12 + C)
            dve.tensor_scalar(q_neg[:, :, 0:CLUSTERS], csum[:], 0.0, None, ALU.is_lt).then_inc(ready, 1)
            dve.wait_ge(ready, 13 + C)
            dve.scalar_tensor_tensor(sigT[:, :, TILES:COLS], csum[:], 0.0, q_neg[:, :, 0:CLUSTERS],
                                     ALU.is_gt, ALU.subtract).then_inc(ready, 1)
            dve.wait_ge(ready, 14 + C)
            dve.wait_ge(setup_a, 2)

            def stats(k, s, src):
                for g in range(G):
                    dve.bn_stats(st[k][:, g, :], src(g)).then_inc(stat[k], 1)
                for g in range(G):
                    dve.wait_ge(stat[k], G * s.n + g + 1)
                    dve.nop(nofuse=True)
                    dve.bn_aggr(mv[k][:, g, :], st[k][:, g, :]).then_inc(mean_var[k], 1)
                dve.wait_ge(mean_var[k], G * s.n + G)
                dve.tensor_scalar(ve[k][:], mv[k][:, :, 1], EPS, None, ALU.add).then_inc(var_eps[k], 1)

            def normalise(k, g, dst, src):
                return dve.tensor_scalar(dst, src, mv[k][:, g, 0:1], rs[k][:, g:g + 1], ALU.subtract, ALU.mult)

            def norm_input(s):
                dve.wait_ge(xa_in[s.u], s.j * 16 + 16)
                stats("a", s, lambda g: xa[s.u][:, g, :])
                dve.wait_ge(rstd["a"], s.n + 1)
                if s.least >= 1:
                    dve.wait_ge(xn_turned, G * s.n)
                for g in range(G):
                    normalise("a", g, xn[:, g, :], xa[s.u][:, g, :]).then_inc(xn_done, 1)

            def mix_input(s, qs):
                dve.wait_ge(dx_done, s.n + 1)
                if s.least >= 2:
                    dve.wait_ge(proj_done, 8 * s.n - 8)
                for q in qs:
                    for c in range(C):
                        dve.scalar_tensor_tensor(mix[s.u][q][:, c, :], dx[:, c, :], vec[:, VEC_MV + q, c:c + 1],
                                                 xnT[s.u][:, c, 0:T], ALU.mult, ALU.add).then_inc(mixed, 1)

            def recur(s, p):
                dve.wait_ge(proj_done, 8 * s.n + 4 * p + K + 1)
                for m in (2 * p, 2 * p + 1):
                    dve.wait_ge(v_done, C * s.n + m + 1)
                    dve.scalar_tensor_tensor(kv[:, m, :], proj_ps[K][:, m % 2, :], vec[:, VEC_BK, m:m + 1],
                                             vS[:, m, :], ALU.add, ALU.mult).then_inc(kv_done, 1)
                for m in (2 * p, 2 * p + 1):
                    dve.wait_ge(kv_done, C * s.n + m + 1)
                    dve.tensor_tensor_scan(acc[s.u][:, m, :], decay[:, m:m + 1].to_broadcast([P, T]), kv[:, m, :],
                                           acc[s.u][:, m, T - 1:T], ALU.mult, ALU.add).then_inc(scan_done, 1)
                for m in (2 * p, 2 * p + 1):
                    dve.wait_ge(scan_done, C * s.n + m + 1)
                    dve.scalar_tensor_tensor(kv[:, m, :], kv[:, m, :], vec[:, VEC_U, m:m + 1],
                                             acc[s.u][:, m, :], ALU.mult, ALU.add).then_inc(wkv_done, 1)

            def receive(s, p):
                dve.wait_ge(proj_done, 8 * s.n + 4 * p + R + 1)
                if s.least >= 2:
                    dve.wait_ge(centered, 2 * s.n - 2)
                for m in (2 * p, 2 * p + 1):
                    dve.wait_ge(wkv_done, C * s.n + m + 1)
                    dve.scalar_tensor_tensor(rw[s.u][:, m, :], proj_ps[R][:, m % 2, :], vec[:, VEC_BR, m:m + 1],
                                             kv[:, m, :], ALU.add, ALU.mult).then_inc(rw_done, 1)

            def route(f):
                links = [0]

                def link(ins):
                    links[0] += 1
                    ins.then_inc(routed, 1)
                    dve.wait_ge(routed, GATE_LINKS * f.n + links[0])

                def best_of(i):
                    dve.wait_ge(ex_done, 2 * f.n + i + 1)
                    link(dve.tensor_scalar(den[:], ex[i][:].rearrange("p g e -> p (g e)"), 1.0, None, ALU.add))
                    link(dve.reciprocal(den[:], den[:]))
                    link(dve.tensor_scalar(pos[:], den[:], float(SEGS), None, ALU.mult))
                    link(dve.tensor_tensor(steps_ge[:], pos[:].unsqueeze(1).to_broadcast([P, KNOTS, E]),
                                           cst[:, CST_FLOOR:CST_FLOOR + KNOTS].unsqueeze(2).to_broadcast([P, KNOTS, E]),
                                           ALU.is_ge))
                    link(dve.tensor_tensor(seg[:], steps_ge[:, 0:SEGS, :], steps_ge[:, 1:KNOTS, :], ALU.subtract))
                    for w in range(3):
                        link(dve.tensor_tensor(pick[:, w, :, :], seg[:],
                                               curve[:, w, :].unsqueeze(2).to_broadcast([P, SEGS, E]), ALU.mult))
                    link(dve.tensor_reduce(piece[:], pick[:].rearrange("p w k e -> p w e k"), X, ALU.add))
                    link(dve.tensor_tensor(pos[:], pos[:], piece[:, 2, :], ALU.subtract))
                    link(dve.tensor_tensor(pos[:], pos[:], piece[:, 1, :], ALU.mult))
                    link(dve.tensor_tensor(val[:].rearrange("p g e -> p (g e)"), piece[:, 0, :], pos[:], ALU.add))
                    link(dve.tensor_reduce(best[:], val[:], X, ALU.max))
                    link(dve.tensor_tensor(is_best[:], val[:], best[:].unsqueeze(2).to_broadcast([P, G, CLUSTERS]),
                                           ALU.is_equal))
                    link(dve.scalar_tensor_tensor(cand[:], is_best[:], -float(CLUSTERS),
                                                  cst[:, CST_IOTA8:CST_IOTA8 + CLUSTERS].unsqueeze(1)
                                                  .to_broadcast([P, G, CLUSTERS]), ALU.mult, ALU.add))
                    link(dve.tensor_reduce(first[:], cand[:], X, ALU.min))
                    link(dve.tensor_tensor(hot[i][:], cst[:, CST_IOTA:CST_IOTA + CLUSTERS].unsqueeze(1)
                                           .to_broadcast([P, G, CLUSTERS]),
                                           first[:].unsqueeze(2).to_broadcast([P, G, CLUSTERS]), ALU.is_equal))

                dve.wait_ge(scores_ps, f.n + 1)
                dve.tensor_scalar(sc[:], turn_ps[:, 0:G * COLS].rearrange("p (g e) -> p g e", g=G),
                                  neg_it[:, 2:3], EXP_MAX, ALU.mult, ALU.min).then_inc(sc_done, 1)
                best_of(0)
                for g in range(G):
                    link(dve.tensor_tensor(prod[:, g, :, :], sc[:, g, 0:TILES].rearrange("p (k t) -> p t k", t=TPC),
                                           hot[0][:, g, :].unsqueeze(1).to_broadcast([P, TPC, CLUSTERS]), ALU.mult))
                link(dve.tensor_reduce(sel[:], prod[:], X, ALU.add))
                assert links[0] == 20
                best_of(1)
                for g in range(G):
                    if f.least >= 1:
                        dve.wait_ge(ohT_ps, f.n)
                    link(dve.tensor_tensor(onehot[:, g, :].rearrange("p (k t) -> p k t", t=TPC),
                                           hot[0][:, g, :].unsqueeze(2).to_broadcast([P, CLUSTERS, TPC]),
                                           hot[1][:, g, :].unsqueeze(1).to_broadcast([P, CLUSTERS, TPC]), ALU.mult))
                assert links[0] == GATE_LINKS

            def magnitude(f):
                links = [0]

                def link(ins):
                    links[0] += 1
                    ins.then_inc(spline, 1)
                    dve.wait_ge(spline, MAG_LINKS * f.n + links[0])

                dve.wait_ge(comp_done, f.n + 1)
                for g, bank in enumerate((turn_ps, side_ps)):
                    dve.wait_ge(tables_ps, G * f.n + g + 1)
                    link(dve.tensor_copy(tS[:, g, :], bank[:, 0:TABLE]))
                link(dve.tensor_tensor(hp[:], tS[:, :, 0:2 * GRID].rearrange("p g (i e) -> p g i e", i=2),
                                       comp[:].unsqueeze(3).to_broadcast([P, G, 2, GRID]), ALU.mult))
                link(dve.tensor_tensor(hh[:], hp[:, :, 0, :], hp[:, :, 1, :], ALU.add))
                link(dve.tensor_tensor(hh[:], hh[:], tS[:, :, 2 * GRID:3 * GRID], ALU.add))
                link(dve.scalar_tensor_tensor(hh[:], hh[:], 0.0, tS[:, :, 3 * GRID:4 * GRID], ALU.max, ALU.mult))
                link(dve.tensor_reduce(mag[:], hh[:], X, ALU.add))
                link(dve.tensor_tensor(mag[:], mag[:], tS[:, :, 4 * GRID], ALU.add))
                link(dve.tensor_scalar(mag[:], mag[:], row[:, ROW_OUTSCALE:ROW_OUTSCALE + 1], None, ALU.mult))
                assert links[0] == MAG_LINKS

            def body(s, do_mix, do_proj, do_norm, do_route):
                a, h, f = s.back(-1), s.back(1), s.back(2)
                if do_mix:
                    norm_input(a)
                if do_proj:
                    recur(s, 0)
                if do_norm:
                    for p in range(2):
                        dve.wait_ge(sq_done, 2 * h.n + p + 1)
                        dve.wait_ge(tg_done, C * h.n + 2 * p + 2)
                        t = tg[h.u][:, 2 * p:2 * p + 2, :].rearrange("p m t -> p (m t)")
                        dve.scalar_tensor_tensor(t, t, 1.0, head_ps[p][:], ALU.add, ALU.mult).then_inc(cg_done, 1)
                if do_proj:
                    receive(s, 0)
                if do_norm:
                    dve.wait_ge(var_done, h.n + 1)
                    if h.least >= 1:
                        dve.wait_ge(head_rs_done, h.n)
                    dve.tensor_scalar(head_ve[:], head_ps[0][0:H, 0:T], 4 * EPS, None,
                                      ALU.add).then_inc(head_ve_done, 1)
                if do_route:
                    route(f)
                if do_proj:
                    recur(s, 1)
                if do_norm:
                    for p in range(2):
                        dve.wait_ge(spread, 2 * h.n + p + 1)
                        dve.wait_ge(cg_done, 2 * h.n + p + 1)
                        if h.least >= 1:
                            dve.wait_ge(wo_done, G * h.n)
                        dve.tensor_tensor(oT[:, 2 * p:2 * p + 2, :].rearrange("p m t -> p (m t)"),
                                          tg[h.u][:, 2 * p:2 * p + 2, :].rearrange("p m t -> p (m t)"),
                                          head_ps[p][:], ALU.mult).then_inc(oT_done, 1)
                if do_mix:
                    mix_input(a, (V, K))
                if do_proj:
                    receive(s, 1)
                if do_norm:
                    dve.wait_ge(wo_done, G * h.n + G)
                    stats("b", h, lambda g: head_ps[g][:])
                if do_mix:
                    mix_input(a, (R, GATE))
                if do_norm:
                    dve.wait_ge(rstd["b"], h.n + 1)
                    if h.least >= 1:
                        dve.wait_ge(x1_done, G * h.n)
                    for g in range(G):
                        normalise("b", g, at[:, g, :], head_ps[g][:]).then_inc(at_done, 1)
                if do_route:
                    magnitude(f)
                    for g, bank in enumerate((turn_ps, side_ps)):
                        dve.wait_ge(dirs_ps, G * f.n + g + 1)
                        if f.least >= 1:
                            dve.wait_ge(fin_done, G * f.n)
                        dve.scalar_tensor_tensor(yb[:, g, :], bank[:], mag[:, g:g + 1], xf[f.u][:, g, :],
                                                 ALU.mult, ALU.add).then_inc(y_done, 1)
                    dve.wait_ge(y_done, G * f.n + G)
                    stats("d", f, lambda g: yb[:, g, :])
                if do_norm:
                    dve.wait_ge(x1_done, G * h.n + G)
                    stats("c", h, lambda g: x1[h.u][:, g, :])
                if do_route:
                    for g in range(G):
                        dve.scalar_tensor_tensor(yb[:, g, :], yb[:, g, :], mv["d"][:, g, 0:1],
                                                 row[:, ROW_GAMMA:ROW_GAMMA + D], ALU.subtract,
                                                 ALU.mult).then_inc(scaled, 1)
                    dve.wait_ge(rstd["d"], f.n + 1)
                    for g in range(G):
                        dve.wait_ge(scaled, G * f.n + g + 1)
                        dve.scalar_tensor_tensor(yb[:, g, :], yb[:, g, :], rs["d"][:, g:g + 1],
                                                 row[:, ROW_BETA:ROW_BETA + D], ALU.mult,
                                                 ALU.add).then_inc(z_done, 1)
                    dve.wait_ge(z_done, G * f.n + G)
                    stats("e", f, lambda g: yb[:, g, :])
                if do_norm:
                    dve.wait_ge(rstd["c"], h.n + 1)
                    if h.least >= 2:
                        dve.wait_ge(xf_turned, G * h.n - G)
                    for g in range(G):
                        normalise("c", g, xf[h.u][:, g, :], x1[h.u][:, g, :]).then_inc(xf_done, 1)
                if do_route:
                    dve.wait_ge(rstd["e"], f.n + 1)
                    for g in range(G):
                        normalise("e", g, yb[:, g, :], yb[:, g, :]).then_inc(zn_done, 1)

            dve.wait_ge(setup_p, 5)
            norm_input(Step(0, 0, 0))
            mix_input(Step(0, 0, 0), range(4))
            schedule(dve, body)


def kernel(L0_attn_x, L0_attn_Wg_w, L0_attn_Wg_b, L0_attn_Wr_w, L0_attn_Wr_b, L0_attn_Wk_w, L0_attn_Wk_b,
           L0_attn_Wv_w, L0_attn_Wv_b, L0_attn_Wo_w, L0_attn_Wo_b, L0_attn_mg, L0_attn_mr, L0_attn_mk,
           L0_attn_mv, L0_attn_w, L0_attn_u, L0_ffn_signatures_raw, L0_ffn_knot_values, L0_ffn_temperature,
           L0_ffn_compress_w1, L0_ffn_compress_b1, L0_ffn_compress_w2, L0_ffn_compress_b2, L0_ffn_spline_w1,
           L0_ffn_spline_b1, L0_ffn_spline_w2, L0_ffn_spline_b2, L0_ffn_directions, L0_ffn_norm_gamma,
           L0_ffn_norm_beta, L0_ffn_output_scale):
    import concourse.bacc as bacc
    from concourse.bass_utils import run_bass_kernel_spmd

    def col(v):
        return np.asarray(v).reshape(C, P).T

    vecs = np.stack([col(v) for v in (L0_attn_mv, L0_attn_mk, L0_attn_mr, L0_attn_mg, L0_attn_Wv_b, L0_attn_Wk_b,
                                      L0_attn_Wr_b, L0_attn_Wg_b, L0_attn_w, L0_attn_u)], axis=1)
    table = np.concatenate([np.asarray(L0_ffn_spline_w1).reshape(TILES, 2 * GRID), np.asarray(L0_ffn_spline_b1),
                            np.asarray(L0_ffn_spline_w2).reshape(TILES, GRID), np.asarray(L0_ffn_spline_b2)], axis=1)
    rows = np.concatenate([np.asarray(v) for v in (L0_ffn_norm_gamma, L0_ffn_norm_beta, L0_ffn_knot_values,
                                                   L0_ffn_temperature, L0_ffn_output_scale)])
    arrays = {
        "x": np.asarray(L0_attn_x),
        "w_proj": np.stack([np.asarray(w).T for w in (L0_attn_Wv_w, L0_attn_Wk_w, L0_attn_Wr_w, L0_attn_Wg_w)]),
        "w_out": np.asarray(L0_attn_Wo_w).T,
        "sig_raw": np.asarray(L0_ffn_signatures_raw).T,
        "comp_w1": np.asarray(L0_ffn_compress_w1),
        "comp_w2": np.asarray(L0_ffn_compress_w2),
        "table": np.concatenate([table] * G),
        "directions": np.concatenate([np.asarray(L0_ffn_directions)] * G),
        "vecs": vecs,
        "comp_b1": np.asarray(L0_ffn_compress_b1).reshape(HID, 1),
        "rows": np.broadcast_to(rows, (P, ROWS)),
        "bias_rows": np.concatenate([np.asarray(L0_attn_Wo_b), np.asarray(L0_ffn_compress_b2)]).reshape(1, D + 2),
        "consts": shape_constants(),
    }
    arrays = {k: np.ascontiguousarray(v) for k, v in arrays.items()}

    nc = bacc.Bacc("TRN2", target_bir_lowering=False, num_devices=1)
    ins = {k: nc.dram_tensor(k, v.shape, mybir.dt.from_np(v.dtype), kind="ExternalInput").ap()
           for k, v in arrays.items()}
    out = nc.dram_tensor("out", (B, N, D), F32, kind="ExternalOutput").ap()
    build(nc, **ins, out=out)
    r = run_bass_kernel_spmd(nc, [arrays], core_ids=[0])
    return r.results[0]["out"]
```

```python
from contextlib import ExitStack
from typing import NamedTuple

import numpy as np

import concourse.bass as bass
from concourse import mybir

P = 128
B, N, D = 2, 8192, 512
H = 16
HD = D // H
C = D // P
G = 2
T = G * P
BLOCKS = N // T
STEPS = B * BLOCKS
TILES, CLUSTERS = 64, 8
TPC = TILES // CLUSTERS
GRID = 16
HID = 128
KNOTS = 8
SEGS = KNOTS - 1
COLS = TILES + CLUSTERS
TABLE = 4 * GRID + 2
EPS = 1e-5
EXP_MAX = 88.5

F32 = mybir.dt.float32
F32R = mybir.dt.float32r
ALU = mybir.AluOpType
ACT = mybir.ActivationFunctionType
X = mybir.AxisListType.X

V, K, R, GATE = range(4)
(VEC_MV, VEC_MK, VEC_MR, VEC_MG, VEC_BV, VEC_BK, VEC_BR, VEC_BG, VEC_W, VEC_U) = range(10)
ROW_GAMMA, ROW_BETA, ROW_KNOTS = 0, D, 2 * D
ROW_TEMP = ROW_KNOTS + KNOTS
ROW_OUTSCALE = ROW_TEMP + 1
ROWS = ROW_OUTSCALE + 1
CST_IDENT = 0
CST_CENTER = CST_IDENT + P
CST_HEADVAR = CST_CENTER + P
CST_FLOOR = CST_HEADVAR + C * H
CST_SEG = CST_FLOOR + KNOTS
CST_IOTA = CST_SEG + SEGS
CST_IOTA8 = CST_IOTA + CLUSTERS
CST_COLS = CST_IOTA8 + CLUSTERS

GATE_LINKS = 40
READY = 14 + C
MAG_LINKS = 9


class Step(NamedTuple):
    j: object
    u: int
    least: int

    @property
    def n(self):
        return self.j * 2 + self.u

    def back(self, k):
        u = (self.u - k) % 2
        return Step(self.j + (self.u - k - u) // 2, u, self.least - k)


def shape_constants():
    c = np.zeros((P, CST_COLS), np.float32)
    spread = np.zeros((2 * H, C * P), np.float32)
    p = np.arange(P)
    same_head = (p[:, None] // HD == p[None, :] // HD)
    c[:, CST_IDENT:CST_IDENT + P] = np.eye(P)
    c[:, CST_CENTER:CST_CENTER + P] = np.eye(P) - same_head / HD
    per = P // HD
    for m in range(C):
        c[p, CST_HEADVAR + m * H + m * per + p // HD] = 4.0 / HD
        for half in range(2):
            spread[half * H + m * per + p // HD, m * P + p] = 1.0
    c[:, CST_FLOOR:CST_FLOOR + KNOTS] = [-1.0] + list(range(1, SEGS)) + [1e30]
    c[:, CST_SEG:CST_SEG + SEGS] = np.arange(SEGS)
    c[:, CST_IOTA:CST_IOTA + CLUSTERS] = np.arange(CLUSTERS)
    c[:, CST_IOTA8:CST_IOTA8 + CLUSTERS] = np.arange(CLUSTERS) + CLUSTERS
    return c, spread


def build(nc, x, w_proj, w_out, sig_raw, comp_w1, comp_w2, table, directions, vecs, comp_b1,
          rows, bias_out, bias_comp, consts, spread_rows, out):
    ctx = ExitStack()
    with ctx:
        def sb(name, shape, dtype=F32):
            return ctx.enter_context(nc.sbuf_tensor(name, shape, dtype))

        def psum(name, shape):
            return ctx.enter_context(nc.psum_tensor(name, shape, F32))

        def sem(name):
            return ctx.enter_context(nc.semaphore(name))

        w_hi = [sb(f"w_hi{q}", [P, C, D], F32R) for q in range(4)]
        w_lo = [sb(f"w_lo{q}", [P, C, D], F32R) for q in range(4)]
        woT = sb("woT", [P, C, D])
        sigT = sb("sigT", [P, C, COLS])
        w1T = sb("w1T", [P, C, HID])
        w2 = sb("w2", [P, 2])
        tabs = sb("tabs", [P, TABLE], F32R)
        dirs = sb("dirs", [P, D], F32R)
        bo = sb("bo", [2 * HD, D], F32R)
        bo_ones = sb("bo_ones", [2 * HD, P], F32R)
        b2 = sb("b2", [1, 2])
        vec = sb("vec", [P, 10, C])
        b1 = sb("b1", [P, 1])
        row = sb("row", [P, ROWS])
        cst = sb("cst", [P, CST_COLS])
        spreader = sb("spreader", [2 * H, C, P], F32R)
        ones = sb("ones", [1, P])
        mhalf = sb("mhalf", [P, G, H])
        expw = sb("expw", [P, C])
        decay = sb("decay", [P, C])
        bg_half = sb("bg_half", [P, C])
        neg_it = sb("neg_it", [P, 3])
        curve = sb("curve", [P, 3, SEGS])
        csum = sb("csum", [P, C, CLUSTERS])
        seed_st = sb("seed_st", [B, 6])
        seed_mv = sb("seed_mv", [B, 2])
        seed_ve = sb("seed_ve", [B, 1])
        seed_rs = sb("seed_rs", [B, 1])
        seed = sb("seed", [P, C, B])

        xa = [sb(f"xa{u}", [P, G, D]) for u in range(2)]
        xnT = [sb(f"xnT{u}", [P, C, T + 1]) for u in range(2)]
        dx = sb("dx", [P, C, T])
        raw_mix = [sb(f"raw_mix{i}", [P, 2, T]) for i in range(4)]
        mix_hi = [sb(f"mix_hi{q}", [P, C, T], F32R) for q in range(4)]
        mix_lo = [sb(f"mix_lo{q}", [P, C, T], F32R) for q in range(4)]
        vS = sb("vS", [P, C, T])
        kv = sb("kv", [P, C, T])
        acc = sb("acc", [P, C, T])
        carry = [sb(f"carry{u}", [P, C]) for u in range(2)]
        rw = sb("rw", [P, C, T])
        tg = sb("tg", [P, C, T])
        sq = sb("sq", [P, C, T])
        head_ve = sb("head_ve", [P, G, H])
        head_rs = sb("head_rs", [P, G, H])
        head_hl = sb("head_hl", [P, G, 2, H], F32R)
        rsT = sb("rsT", [2 * H, T], F32R)
        oT = sb("oT", [P, C, T])
        at = sq[:].rearrange("p c t -> p (c t)").rearrange("p (g d) -> p g d", g=G)
        x1 = [sb(f"x1_{u}", [P, G, D]) for u in range(2)]
        xf = [sb(f"xf{u}", [P, G, D]) for u in range(2)]
        xfT = oT
        yb = sb("yb", [P, G, D])
        st = {k: sb(f"st_{k}", [P, G, 6]) for k in "abcde"}
        mv = {k: sb(f"mv_{k}", [P, G, 2]) for k in "abcde"}
        ve = {k: sb(f"ve_{k}", [P, G]) for k in "abcde"}
        rs = {k: sb(f"rs_{k}", [P, G]) for k in "abcde"}
        nb = {k: sb(f"nb_{k}", [P, G]) for k in "abcde"}
        sc = sb("sc", [P, G, COLS])
        hS = sb("hS", [P, T])
        ex = [sb(f"ex{i}", [P, G, CLUSTERS]) for i in range(2)]
        E = G * CLUSTERS
        sel = sb("sel", [P, G, TPC])
        den = sb("den", [P, E])
        pos = sb("pos", [P, E])
        steps_ge = sb("steps_ge", [P, KNOTS, E])
        seg = sb("seg", [P, SEGS, E])
        pick = sb("pick", [P, 3, SEGS, E])
        piece = sb("piece", [P, 3, E])
        val = sb("val", [P, G, CLUSTERS])
        best = sb("best", [P, G])
        is_best = sb("is_best", [P, G, CLUSTERS])
        cand = sb("cand", [P, G, CLUSTERS])
        first = sb("first", [P, G])
        hot = [sb(f"hot{i}", [P, G, CLUSTERS]) for i in range(2)]
        prod = sb("prod", [P, G, TPC, CLUSTERS])
        onehot = sb("onehot", [P, G, 2, TILES])
        ohT = sb("ohT", [P, T], F32R)
        comp = sb("comp", [P, G, 2])
        tS = sb("tS", [P, G, TABLE])
        hp = sb("hp", [P, G, 2, GRID])
        hh = sb("hh", [P, G, GRID])
        mag = sb("mag", [P, G])

        seed_x = xf[0][0:B, 0, :]
        seed_xn = tg[0:B, 0:2, :].rearrange("p c t -> p (c t)")
        raw = kv[:, :, 0:TILES]
        q_pos = vS[:, :, 0:TILES]
        q_neg = acc[:, :, 0:TILES]
        spreader_in = tg[0:2 * H, 2:4, :].rearrange("p c t -> p (c t)")
        dirs_in = rw[:, 0:2, :].rearrange("p c t -> p (c t)")
        tabs_in = rw[:, 2, 0:TABLE]
        bo_in = dx[0:2 * HD, 0:2, :].rearrange("p c t -> p (c t)")
        w_in = [[x1[0][:], x1[1][:]], [yb[:], at], [xf[1][:], oT[:].rearrange("p c t -> p (c t)").rearrange(
            "p (g d) -> p g d", g=G)], [x1[0][:], x1[1][:]]]

        proj_ps = [psum(f"proj_ps{i}", [P, 2, T]) for i in range(4)]
        turn_ps = psum("turn_ps", [P, 512])
        head_ps = [psum(f"head_ps{p}", [P, 512]) for p in range(2)]
        side_ps = psum("side_ps", [P, 512])

        weights_in = sem("weights_in")
        wo_in = sem("wo_in")
        w_half_in = [sem(f"w_half_in{q}") for q in range(4)]
        w_hi_done = sem("w_hi_done")
        w_lo_done = sem("w_lo_done")
        xa_in = [sem(f"xa_in{u}") for u in range(2)]
        xr_in = [sem(f"xr_in{u}") for u in range(2)]
        stored = [sem(f"stored{u}") for u in range(2)]
        setup_v = sem("setup_v")
        setup_a = sem("setup_a")
        setup_p = sem("setup_p")
        setup_t = sem("setup_t")
        ready = sem("ready")
        stat = {k: sem(f"stat_{k}") for k in "abcde"}
        mean_var = {k: sem(f"mean_var_{k}") for k in "abcde"}
        var_eps = {k: sem(f"var_eps_{k}") for k in "abcde"}
        rstd = {k: sem(f"rstd_{k}") for k in "abcde"}
        biased = {k: sem(f"biased_{k}") for k in "abcde"}
        xn_done = sem("xn_done")
        xn_turned = sem("xn_turned")
        xnT_done = sem("xnT_done")
        dx_done = sem("dx_done")
        raw_done = [sem(f"raw_done{q}") for q in range(4)]
        hi_done = [sem(f"hi_done{q}") for q in range(4)]
        lo_done = [sem(f"lo_done{q}") for q in range(4)]
        proj_done = sem("proj_done")
        v_done = sem("v_done")
        kv_done = sem("kv_done")
        scan_done = sem("scan_done")
        carried = sem("carried")
        wkv_done = sem("wkv_done")
        rw_done = sem("rw_done")
        tg_done = sem("tg_done")
        centered = sem("centered")
        sq_done = sem("sq_done")
        cg_done = sem("cg_done")
        var_done = sem("var_done")
        head_ve_done = sem("head_ve_done")
        head_rs_done = sem("head_rs_done")
        head_hi = sem("head_hi")
        head_lo = sem("head_lo")
        rs_turned = sem("rs_turned")
        rsT_done = sem("rsT_done")
        spread = sem("spread")
        oT_done = sem("oT_done")
        wo_done = sem("wo_done")
        at_done = sem("at_done")
        x1_done = sem("x1_done")
        xf_done = sem("xf_done")
        xf_turned = sem("xf_turned")
        xfT_done = sem("xfT_done")
        hidden_ps = sem("hidden_ps")
        scores_ps = sem("scores_ps")
        sc_done = sem("sc_done")
        ex_done = sem("ex_done")
        routed = sem("routed")
        hS_done = sem("hS_done")
        comp_ps = sem("comp_ps")
        comp_done = sem("comp_done")
        ohT_ps = sem("ohT_ps")
        ohT_done = sem("ohT_done")
        tables_ps = sem("tables_ps")
        spline = sem("spline")
        dirs_ps = sem("dirs_ps")
        y_done = sem("y_done")
        yn_done = sem("yn_done")
        scaled = sem("scaled")
        z_done = sem("z_done")
        zn_done = sem("zn_done")
        fin_done = sem("fin_done")

        x_t = x.rearrange("s (j g p) d -> s j p g d", g=G, p=P)
        out_t = out.rearrange("s (j g p) d -> s j p g d", g=G, p=P)
        ident = cst[:, CST_IDENT:CST_IDENT + P]
        center = cst[:, CST_CENTER:CST_CENTER + P]
        N_WEIGHTS = 13

        def schedule(eng, body):
            body(Step(0, 0, 0), True, True, False, False, False)
            body(Step(0, 1, 1), True, True, True, False, False)
            body(Step(1, 0, 2), True, True, True, True, False)
            body(Step(1, 1, 3), True, True, True, True, True)
            with eng.Fori(2, BLOCKS - 1) as j:
                for u in range(2):
                    body(Step(j, u, 4 + u), True, True, True, True, True)
            j = BLOCKS - 1
            body(Step(j, 0, 2 * j), True, True, True, True, True)
            body(Step(j, 1, 2 * j + 1), False, True, True, True, True)
            body(Step(j + 1, 0, 2 * j + 2), False, False, True, True, True)
            body(Step(j + 1, 1, 2 * j + 3), False, False, False, True, True)
            body(Step(j + 2, 0, 2 * j + 4), False, False, False, False, True)

        def split_low(eng, s, q, i):
            eng.wait_ge(hi_done[q], 2 * s.n + i + 1)
            if s.least >= 1:
                eng.wait_ge(proj_done, 8 * s.n - 8 + 2 * q + 2)
            cs = slice(2 * i, 2 * i + 2)
            eng.tensor_tensor(mix_lo[q][:, cs, :], raw_mix[(2 * q + i) % 4][:], mix_hi[q][:, cs, :].bitcast(F32),
                              ALU.subtract).then_inc(lo_done[q], 1)

        block = ctx.enter_context(nc.Block())

        @block.sync
        def _(sp):
            for u in range(2):
                sp.dma_start(xa[u][:], x_t[u, 0]).then_inc(xa_in[u], 16)
            sp.dma_start(seed_x, x[:, N - 1, :]).then_inc(weights_in, 16)
            sp.dma_start(cst[:], consts).then_inc(weights_in, 16)
            sp.dma_start(spreader_in, spread_rows).then_inc(weights_in, 16)
            sp.dma_start(vec[:], vecs).then_inc(weights_in, 16)
            sp.dma_start(raw, sig_raw.rearrange("(c p) o -> p c o", p=P)).then_inc(weights_in, 16)
            sp.dma_start(w1T[:], comp_w1.rearrange("(c p) o -> p c o", p=P)).then_inc(weights_in, 16)
            sp.dma_start(w2[:], comp_w2).then_inc(weights_in, 16)
            sp.dma_start(tabs_in, table).then_inc(weights_in, 16)
            sp.dma_start(dirs_in, directions).then_inc(weights_in, 16)
            sp.dma_start(b1[:], comp_b1).then_inc(weights_in, 16)
            sp.dma_start(b2[:], bias_comp).then_inc(weights_in, 16)
            sp.dma_start(bo_in, bias_out).then_inc(weights_in, 16)
            sp.dma_start(row[:], rows).then_inc(weights_in, 16)
            for q in range(4):
                if q == 3:
                    sp.wait_ge(w_lo_done, 2)
                halves = w_proj[q].rearrange("(i c p) o -> i p c o", i=2, p=P)
                for i in range(2):
                    sp.dma_start(w_in[q][i], halves[i]).then_inc(w_half_in[q], 16)
            sp.dma_start(woT[:], w_out.rearrange("(c p) o -> p c o", p=P)).then_inc(wo_in, 16)

            def body(s, do_mix, do_proj, do_norm, do_route, do_end):
                h, e = s.back(1), s.back(3)
                if do_mix and s.least + 2 < STEPS and do_proj:
                    sp.wait_ge(xn_turned, G * s.n + G)
                    sp.nop(nofuse=True)
                    sp.dma_start(xa[s.u][:], x_t[s.u, s.j + 1]).then_inc(xa_in[s.u], 16)
                if do_end:
                    sp.wait_ge(fin_done, G * e.n + G)
                    sp.nop(nofuse=True)
                    sp.dma_start(out_t[e.u, e.j], x1[e.u][:]).then_inc(stored[e.u], 16)
                if do_norm:
                    if h.least < 2:
                        sp.wait_ge(w_lo_done, 8)
                    if h.least >= 2:
                        sp.wait_ge(stored[h.u], h.j * 16)
                        sp.nop(nofuse=True)
                    sp.dma_start(x1[h.u][:], x_t[h.u, h.j]).then_inc(xr_in[h.u], 16)

            schedule(sp, body)
            for u in range(2):
                sp.wait_ge(stored[u], 16 * BLOCKS)

        @block.gpsimd
        def _(pool):
            pool.memset(mhalf[:], -0.5).then_inc(setup_p, 1)
            pool.memset(ones[:], 1.0).then_inc(setup_p, 1)
            for u in range(2):
                pool.memset(carry[u][:], 0.0).then_inc(setup_p, 1)
            pool.memset(bo[:].bitcast(F32), 0.0).then_inc(setup_p, 1)
            pool.memset(bo_ones[:].bitcast(F32), 1.0).then_inc(setup_p, 1)
            pool.wait_ge(setup_p, 6)
            pool.wait_ge(setup_v, 3)
            pool.tensor_tensor(seed_rs[:], seed_ve[:], mhalf[0:B, 0, 0:1], ALU.pow).then_inc(setup_p, 1)

            def root(k, s):
                pool.wait_ge(var_eps[k], s.n + 1)
                pool.tensor_tensor(rs[k][:], ve[k][:], mhalf[:, 0, 0:G], ALU.pow).then_inc(rstd[k], 1)

            def delta(s):
                pool.wait_ge(xnT_done, 3 * s.n + 3)
                if s.least >= 1:
                    pool.wait_ge(raw_done[GATE], 2 * s.n)
                pool.tensor_tensor(dx[:], xnT[s.u][:, :, 1:T + 1], xnT[s.u][:, :, 0:T],
                                   ALU.subtract).then_inc(dx_done, 1)

            def low_part(s, q):
                for i in range(2):
                    split_low(pool, s, q, i)

            def body(s, do_mix, do_proj, do_norm, do_route, do_end):
                a, h, f, e = (s.back(k) for k in (-1, 1, 2, 3))
                if do_mix:
                    root("a", a)
                if do_proj:
                    low_part(s, GATE)
                if do_end:
                    root("d", e)
                if do_norm:
                    pool.wait_ge(head_ve_done, h.n + 1)
                    pool.tensor_tensor(head_rs[:], head_ve[:], mhalf[:], ALU.pow).then_inc(head_rs_done, 1)
                if do_end:
                    for g in range(G):
                        pool.wait_ge(scaled, G * e.n + g + 1)
                        pool.tensor_tensor(yb[:, g, :], yb[:, g, :], row[:, ROW_BETA:ROW_BETA + D],
                                           ALU.add).then_inc(z_done, 1)
                if do_mix:
                    delta(a)
                if do_end:
                    root("e", e)
                    for g in range(G):
                        pool.wait_ge(zn_done, G * e.n + g + 1)
                        pool.tensor_tensor(x1[e.u][:, g, :], x1[e.u][:, g, :], yb[:, g, :],
                                           ALU.add).then_inc(fin_done, 1)
                if do_mix:
                    low_part(a, K)
                if do_norm:
                    root("b", h)
                    pool.wait_ge(xr_in[h.u], h.j * 16 + 16)
                    for g in range(G):
                        pool.wait_ge(at_done, G * h.n + g + 1)
                        pool.tensor_tensor(x1[h.u][:, g, :], x1[h.u][:, g, :], at[:, g, :],
                                           ALU.add).then_inc(x1_done, 1)
                    root("c", h)

            first_step = Step(0, 0, 0)
            root("a", first_step)
            pool.wait_ge(ready, READY + 3)
            delta(first_step)
            low_part(first_step, K)
            schedule(pool, body)

        @block.scalar
        def _(act):
            act.wait_ge(weights_in, 16 * N_WEIGHTS)
            act.activation(expw[:], vec[:, VEC_W, :], ACT.Exp).then_inc(setup_a, 1)
            act.wait_ge(setup_a, 1)
            act.activation(decay[:], expw[:], ACT.Exp, scale=-1.0).then_inc(setup_a, 1)
            act.wait_ge(setup_t, 1)
            act.activation(seed[:], turn_ps[:, 0:C * B].rearrange("p (c s) -> p c s", c=C),
                           ACT.Copy).then_inc(setup_a, 1)
            act.wait_ge(setup_a, 3)
            act.wait_ge(ready, READY)
            act.activation(dirs[:], dirs_in, ACT.Copy).then_inc(setup_a, 1)
            act.activation(tabs[:], tabs_in, ACT.Copy).then_inc(setup_a, 1)
            act.wait_ge(setup_p, 6)
            for p0 in (0, HD):
                act.activation(bo[p0:p0 + 1, :], bo_in[p0:p0 + 1, :], ACT.Copy).then_inc(setup_a, 1)
            act.activation(spreader[:], spreader_in.rearrange("p (c k) -> p c k", c=C), ACT.Copy).then_inc(setup_a, 1)
            for q in range(4):
                act.wait_ge(w_half_in[q], 32)
                for i in range(2):
                    act.activation(w_hi[q][:, 2 * i:2 * i + 2, :], w_in[q][i], ACT.Copy).then_inc(w_hi_done, 1)

            def rows_by(k, s, g, dst, src, done):
                act.wait_ge(biased[k], s.n + 1)
                act.activation(dst, src, ACT.Identity, scale=rs[k][:, g:g + 1],
                               bias=nb[k][:, g:g + 1]).then_inc(done, 1)

            def norm_input(s):
                for g in range(G):
                    rows_by("a", s, g, xa[s.u][:, g, :], xa[s.u][:, g, :], xn_done)

            def high_part(s, q):
                for i in range(2):
                    act.wait_ge(raw_done[q], 2 * s.n + i + 1)
                    if s.least >= 1:
                        act.wait_ge(proj_done, 8 * s.n - 8 + 2 * q + 2)
                        act.wait_ge(lo_done[q], 2 * s.n - 1 + i)
                    act.activation(mix_hi[q][:, 2 * i:2 * i + 2, :], raw_mix[(2 * q + i) % 4][:],
                                   ACT.Copy).then_inc(hi_done[q], 1)

            def turned_input(s):
                if s.least >= 2:
                    act.wait_ge(raw_done[GATE], 2 * s.n - 2)
                    act.wait_ge(dx_done, s.n - 1)
                before = xnT[s.u][:, :, T:T + 1] if s.least >= 2 else seed[:, :, s.u:s.u + 1]
                act.activation(xnT[s.u][:, :, 0:1], before, ACT.Copy).then_inc(xnT_done, 1)
                act.wait_ge(xnT_done, 3 * s.n + 1)
                for g in range(G):
                    act.wait_ge(xn_turned, G * s.n + g + 1)
                    act.activation(xnT[s.u][:, :, 1 + g * P:1 + g * P + P],
                                   turn_ps[:].rearrange("p (c t) -> p c t", c=C), ACT.Copy).then_inc(xnT_done, 1)

            def values(s, p):
                act.wait_ge(proj_done, 8 * s.n + 2 * V + p + 1)
                for i in range(2):
                    m = 2 * p + i
                    if s.least >= 1:
                        act.wait_ge(kv_done, C * s.n - C + m + 1)
                    act.activation(vS[:, m, :], proj_ps[p][:, i, :], ACT.Identity,
                                   bias=vec[:, VEC_BV, m:m + 1]).then_inc(v_done, 1)

            def gates(s, p):
                act.wait_ge(proj_done, 8 * s.n + 2 * GATE + p + 1)
                if s.least >= 1:
                    act.wait_ge(oT_done, 2 * s.n)
                for i in range(2):
                    m = 2 * p + i
                    act.activation(tg[:, m, :], proj_ps[2 + p][:, i, :], ACT.Tanh, scale=0.5,
                                   bias=bg_half[:, m:m + 1]).then_inc(tg_done, 1)

            def body(s, do_mix, do_proj, do_norm, do_route, do_end):
                a, h, f, e = (s.back(k) for k in (-1, 1, 2, 3))
                if do_proj:
                    values(s, 0)
                    values(s, 1)
                    high_part(s, GATE)
                if do_norm:
                    for p in range(2):
                        act.wait_ge(centered, 2 * h.n + p + 1)
                        if h.least >= 1:
                            act.wait_ge(x1_done, G * h.n)
                        act.activation(sq[:, 2 * p:2 * p + 2, :],
                                       head_ps[p][:].rearrange("p (m t) -> p m t", m=2),
                                       ACT.Square).then_inc(sq_done, 1)
                if do_mix:
                    norm_input(a)
                if do_end:
                    for g in range(G):
                        rows_by("d", e, g, yb[:, g, :], yb[:, g, :], yn_done)
                if do_route:
                    act.wait_ge(wo_done, G * f.n + G)
                    for g, bank in enumerate((turn_ps, side_ps)):
                        act.wait_ge(xf_turned, G * f.n + g + 1)
                        act.activation(xfT[:, :, g * P:g * P + P],
                                       bank[:].rearrange("p (c t) -> p c t", c=C), ACT.Copy).then_inc(xfT_done, 1)
                    act.wait_ge(sc_done, f.n + 1)
                    act.activation(ex[0][:], sc[:, :, TILES:COLS], ACT.Exp).then_inc(ex_done, 1)
                if do_mix:
                    turned_input(a)
                if do_route:
                    act.wait_ge(routed, GATE_LINKS * f.n + 20)
                    act.activation(ex[1][:], sel[:], ACT.Exp).then_inc(ex_done, 1)
                if do_norm:
                    act.wait_ge(rs_turned, h.n + 1)
                    if h.least >= 1:
                        act.wait_ge(spread, 2 * h.n)
                    act.activation(rsT[:], head_ps[1][0:2 * H, 0:T], ACT.Copy).then_inc(rsT_done, 1)
                if do_route:
                    act.wait_ge(hidden_ps, f.n + 1)
                    if f.least >= 1:
                        act.wait_ge(comp_ps, f.n)
                    act.activation(hS[:], side_ps[:, 0:T], ACT.Gelu, bias=b1[:, 0:1]).then_inc(hS_done, 1)
                if do_mix:
                    high_part(a, V)
                if do_end:
                    for g in range(G):
                        rows_by("e", e, g, yb[:, g, :], yb[:, g, :], zn_done)
                if do_route:
                    act.wait_ge(comp_ps, f.n + 1)
                    if f.least >= 1:
                        act.wait_ge(spline, MAG_LINKS * f.n)
                    act.activation(comp[:], side_ps[:, 0:2 * G].rearrange("p (g o) -> p g o", g=G),
                                   ACT.Tanh).then_inc(comp_done, 1)
                if do_mix:
                    high_part(a, K)
                if do_proj:
                    gates(s, 0)
                if do_mix:
                    high_part(a, R)
                if do_norm:
                    for g in range(G):
                        rows_by("b", h, g, at[:, g, :], head_ps[g][:], at_done)
                if do_proj:
                    gates(s, 1)
                if do_route:
                    act.wait_ge(ohT_ps, f.n + 1)
                    if f.least >= 1:
                        act.wait_ge(dirs_ps, G * f.n)
                    act.activation(ohT[:], turn_ps[:, 0:T], ACT.Copy).then_inc(ohT_done, 1)
                if do_norm:
                    if h.least >= 2:
                        act.wait_ge(xf_turned, G * h.n - G)
                        act.wait_ge(y_done, G * h.n - G)
                    for g in range(G):
                        rows_by("c", h, g, xf[h.u][:, g, :], x1[h.u][:, g, :], xf_done)

            first_step = Step(0, 0, 0)
            norm_input(first_step)
            turned_input(first_step)
            act.wait_ge(w_lo_done, 8)
            for q in (V, K, R):
                high_part(first_step, q)
            schedule(act, body)

        @block.tensor
        def _(pe):
            pe.wait_ge(weights_in, 16 * N_WEIGHTS)
            pe.wait_ge(setup_v, 4)
            for c in range(C):
                last = pe.transpose(turn_ps[:, c * B:c * B + B], seed_xn[:, c * P:c * P + P], ident[0:B, 0:B])
            last.then_inc(setup_t, 1)
            pe.wait_ge(setup_a, 3)

            def turn_input(s, g):
                pe.wait_ge(xn_done, G * s.n + g + 1)
                if g or s.least >= 1:
                    pe.wait_ge(xnT_done, 3 * s.n + 2 * g)
                for c in range(C):
                    last = pe.transpose(turn_ps[:, c * P:c * P + P], xa[s.u][:, g, c * P:c * P + P], ident)
                last.then_inc(xn_turned, 1)

            def project(s, q, p):
                pe.wait_ge(hi_done[q], 2 * s.n + 2)
                pe.wait_ge(lo_done[q], 2 * s.n + 2)
                if q == V and s.least >= 1:
                    pe.wait_ge(rw_done, C * s.n - C + 2 * p + 2)
                if q == K and s.least >= 1:
                    pe.wait_ge(tg_done, C * s.n - C + 2 * p + 2)
                if q == R:
                    pe.wait_ge(v_done, C * s.n + 2 * p + 2)
                if q == GATE:
                    pe.wait_ge(kv_done, C * s.n + 2 * p + 2)
                bank = proj_ps[2 * (q % 2) + p]
                for i in range(2):
                    m = 2 * p + i
                    for c in range(C):
                        cols = slice(m * P, m * P + P)
                        pe.matmul(bank[:, i, :], w_hi[q][:, c, cols], mix_hi[q][:, c, :], start=(c == 0), stop=False)
                        pe.matmul(bank[:, i, :], w_hi[q][:, c, cols], mix_lo[q][:, c, :], start=False, stop=False)
                        last = pe.matmul(bank[:, i, :], w_lo[q][:, c, cols], mix_hi[q][:, c, :],
                                         start=False, stop=(c == C - 1))
                last.then_inc(proj_done, 1)

            def body(s, do_mix, do_proj, do_norm, do_route, do_end):
                a, h, f, e = (s.back(k) for k in (-1, 1, 2, 3))
                if do_proj:
                    project(s, V, 0)
                    project(s, V, 1)
                if do_end:
                    pe.wait_ge(comp_done, e.n + 1)
                    pe.wait_ge(ohT_done, e.n + 1)
                    for g, bank in enumerate((turn_ps, side_ps)):
                        pe.matmul(bank[:, 0:TABLE], ohT[:, g * P:g * P + P], tabs[:],
                                  start=True, stop=True).then_inc(tables_ps, 1)
                if do_norm:
                    for p in range(2):
                        pe.wait_ge(rw_done, C * h.n + 2 * p + 2)
                        if h.least >= 1:
                            pe.wait_ge(at_done, G * h.n)
                        for i in range(2):
                            last = pe.matmul(head_ps[p][:, i * T:i * T + T], center, rw[:, 2 * p + i, :],
                                             start=True, stop=True)
                        last.then_inc(centered, 1)
                if do_end:
                    for g, bank in enumerate((turn_ps, side_ps)):
                        pe.wait_ge(spline, MAG_LINKS * e.n + 1 + g)
                        pe.matmul(bank[:], ohT[:, g * P:g * P + P], dirs[:], start=True, stop=True).then_inc(dirs_ps, 1)
                if do_proj:
                    project(s, K, 0)
                if do_norm:
                    pe.wait_ge(sq_done, 2 * h.n + 2)
                    pe.wait_ge(cg_done, 2 * h.n + 1)
                    for g in range(G):
                        for m in range(C):
                            last = pe.matmul(head_ps[0][:, g * H:g * H + H], sq[:, m, g * P:g * P + P],
                                             cst[:, CST_HEADVAR + m * H:CST_HEADVAR + m * H + H],
                                             start=(m == 0), stop=(m == C - 1))
                    last.then_inc(var_done, 1)
                if do_route:
                    for g, bank in enumerate((turn_ps, side_ps)):
                        pe.wait_ge(xf_done, G * f.n + g + 1)
                        pe.wait_ge(xnT_done, (3 * s.n + 3) if do_proj else 3 * STEPS)
                        if do_end:
                            pe.wait_ge(y_done, G * e.n + g + 1)
                        for c in range(C):
                            last = pe.transpose(bank[:, c * P:c * P + P], xf[f.u][:, g, c * P:c * P + P], ident)
                        last.then_inc(xf_turned, 1)
                if do_proj:
                    project(s, K, 1)
                if do_route:
                    pe.wait_ge(xfT_done, G * f.n + G)
                    for g in range(G):
                        for c in range(C):
                            last = pe.matmul(turn_ps[:, g * COLS:g * COLS + COLS], xfT[:, c, g * P:g * P + P],
                                             sigT[:, c, :], start=(c == 0), stop=(c == C - 1))
                    last.then_inc(scores_ps, 1)
                    for c in range(C):
                        last = pe.matmul(side_ps[:, 0:T], w1T[:, c, :], xfT[:, c, :],
                                         start=(c == 0), stop=(c == C - 1))
                    last.then_inc(hidden_ps, 1)
                if do_mix:
                    if do_route:
                        pe.wait_ge(sc_done, f.n + 1)
                    turn_input(a, 0)
                if do_proj:
                    project(s, R, 0)
                if do_mix:
                    turn_input(a, 1)
                if do_proj:
                    project(s, R, 1)
                if do_norm:
                    pe.wait_ge(head_lo, h.n + 1)
                    pe.wait_ge(cg_done, 2 * h.n + 2)
                    for g in range(G):
                        last = pe.transpose(head_ps[1][0:2 * H, g * P:g * P + P],
                                            head_hl[:, g, :, :].rearrange("p i h -> p (i h)").bitcast(F32), ident)
                    last.then_inc(rs_turned, 1)
                    pe.wait_ge(rsT_done, h.n + 1)
                    for p in range(2):
                        for i in range(2):
                            m = 2 * p + i
                            last = pe.matmul(head_ps[p][:, i * T:i * T + T], spreader[:, m, :], rsT[:],
                                             start=True, stop=True)
                        last.then_inc(spread, 1)
                if do_route:
                    pe.wait_ge(hS_done, f.n + 1)
                    for g in range(G):
                        pe.matmul(side_ps[:, 2 * g:2 * g + 2], hS[:, g * P:g * P + P], w2[:], start=True, stop=False)
                        last = pe.matmul(side_ps[:, 2 * g:2 * g + 2], ones[:], b2[:], start=False, stop=True)
                    last.then_inc(comp_ps, 1)
                if do_proj:
                    project(s, GATE, 0)
                if do_norm:
                    pe.wait_ge(oT_done, 2 * h.n + 2)
                    for g in range(G):
                        pe.matmul(head_ps[g][:], bo_ones[:], bo[:], start=True, stop=False)
                        for c in range(C):
                            last = pe.matmul(head_ps[g][:], oT[:, c, g * P:g * P + P], woT[:, c, :],
                                             start=False, stop=(c == C - 1))
                        last.then_inc(wo_done, 1)
                if do_proj:
                    project(s, GATE, 1)
                if do_route:
                    pe.wait_ge(routed, GATE_LINKS * f.n + GATE_LINKS)
                    if do_mix:
                        pe.wait_ge(xnT_done, 3 * a.n + 3)
                    for g in range(G):
                        last = pe.transpose(turn_ps[:, g * P:g * P + P],
                                            onehot[:, g, :, :].rearrange("p i e -> p (i e)"), ident)
                    last.then_inc(ohT_ps, 1)

            first_step = Step(0, 0, 0)
            turn_input(first_step, 0)
            turn_input(first_step, 1)
            pe.wait_ge(w_lo_done, 8)
            pe.wait_ge(ready, READY + 4)
            pe.wait_ge(wo_in, 16)
            schedule(pe, body)

        @block.vector
        def _(dve):
            dve.wait_ge(weights_in, 16 * N_WEIGHTS)
            dve.bn_stats(seed_st[:], seed_x).then_inc(setup_v, 1)
            dve.wait_ge(setup_v, 1)
            dve.bn_aggr(seed_mv[:], seed_st[:]).then_inc(setup_v, 1)
            dve.wait_ge(setup_v, 2)
            dve.tensor_scalar(seed_ve[:], seed_mv[:, 1:2], EPS, None, ALU.add).then_inc(setup_v, 1)
            dve.wait_ge(setup_p, 7)
            dve.tensor_scalar(seed_xn, seed_x, seed_mv[:, 0:1], seed_rs[:], ALU.subtract,
                              ALU.mult).then_inc(setup_v, 1)
            dve.tensor_scalar(neg_it[:, 0:1], row[:, ROW_TEMP:ROW_TEMP + 1], 1e-6, None, ALU.add).then_inc(ready, 1)
            dve.wait_ge(ready, 1)
            dve.reciprocal(neg_it[:, 1:2], neg_it[:, 0:1]).then_inc(ready, 1)
            dve.wait_ge(ready, 2)
            dve.tensor_scalar(neg_it[:, 2:3], neg_it[:, 1:2], -1.0, None, ALU.mult).then_inc(ready, 1)
            dve.tensor_scalar(bg_half[:], vec[:, VEC_BG, :], 0.5, None, ALU.mult).then_inc(ready, 1)
            dve.tensor_copy(curve[:, 0, :], row[:, ROW_KNOTS:ROW_KNOTS + SEGS]).then_inc(ready, 1)
            dve.tensor_tensor(curve[:, 1, :], row[:, ROW_KNOTS + 1:ROW_KNOTS + KNOTS],
                              row[:, ROW_KNOTS:ROW_KNOTS + SEGS], ALU.subtract).then_inc(ready, 1)
            dve.tensor_copy(curve[:, 2, :], cst[:, CST_SEG:CST_SEG + SEGS]).then_inc(ready, 1)
            dve.tensor_scalar(q_pos, raw, 0.3, None, ALU.is_gt).then_inc(ready, 1)
            dve.tensor_scalar(q_neg, raw, -0.3, None, ALU.is_lt).then_inc(ready, 1)
            dve.wait_ge(ready, 9)
            dve.tensor_tensor(q_pos, q_pos, q_neg, ALU.subtract).then_inc(ready, 1)
            dve.wait_ge(ready, 10)
            dve.tensor_tensor(q_pos, q_pos, raw, ALU.subtract).then_inc(ready, 1)
            dve.wait_ge(ready, 11)
            dve.tensor_tensor(sigT[:, :, 0:TILES], raw, q_pos, ALU.add).then_inc(ready, 1)
            dve.wait_ge(ready, 12)
            for c in range(C):
                dve.tensor_reduce(csum[:, c, :], sigT[:, c, 0:TILES].rearrange("p (k t) -> p k t", k=CLUSTERS),
                                  X, ALU.add).then_inc(ready, 1)
            dve.wait_ge(ready, 12 + C)
            dve.tensor_scalar(q_neg[:, :, 0:CLUSTERS], csum[:], 0.0, None, ALU.is_lt).then_inc(ready, 1)
            dve.wait_ge(ready, 13 + C)
            dve.scalar_tensor_tensor(sigT[:, :, TILES:COLS], csum[:], 0.0, q_neg[:, :, 0:CLUSTERS],
                                     ALU.is_gt, ALU.subtract).then_inc(ready, 1)
            dve.wait_ge(ready, READY)
            dve.wait_ge(setup_a, 8)
            above = slice(TILES, P)
            dve.tensor_tensor(dirs[above, :], dirs_in[above, :], dirs[above, :].bitcast(F32),
                              ALU.subtract).then_inc(ready, 1)
            dve.tensor_tensor(tabs[above, :], tabs_in[above, :], tabs[above, :].bitcast(F32),
                              ALU.subtract).then_inc(ready, 1)
            dve.tensor_tensor(bo[HD:HD + 1, :], bo_in[HD:HD + 1, :], bo[HD:HD + 1, :].bitcast(F32),
                              ALU.subtract).then_inc(ready, 1)
            dve.tensor_copy(carry[0][:], carry[0][:]).then_inc(ready, 1)
            for q in range(4):
                for i in range(2):
                    dve.wait_ge(w_hi_done, 2 * q + i + 1)
                    dve.tensor_tensor(w_lo[q][:, 2 * i:2 * i + 2, :], w_in[q][i],
                                      w_hi[q][:, 2 * i:2 * i + 2, :].bitcast(F32), ALU.subtract).then_inc(w_lo_done, 1)

            def stats(k, s, src):
                for g in range(G):
                    dve.bn_stats(st[k][:, g, :], src(g)).then_inc(stat[k], 1)
                for g in range(G):
                    dve.wait_ge(stat[k], G * s.n + g + 1)
                    dve.nop(nofuse=True)
                    dve.bn_aggr(mv[k][:, g, :], st[k][:, g, :]).then_inc(mean_var[k], 1)
                dve.wait_ge(mean_var[k], G * s.n + G)
                dve.tensor_scalar(ve[k][:], mv[k][:, :, 1], EPS, None, ALU.add).then_inc(var_eps[k], 1)

            def bias(k, s):
                dve.wait_ge(rstd[k], s.n + 1)
                dve.scalar_tensor_tensor(nb[k][:], mv[k][:, :, 0], -1.0, rs[k][:], ALU.mult,
                                         ALU.mult).then_inc(biased[k], 1)

            def stats_input(s):
                dve.wait_ge(xa_in[s.u], s.j * 16 + 16)
                stats("a", s, lambda g: xa[s.u][:, g, :])

            def mix_input(s, q):
                dve.wait_ge(dx_done, s.n + 1)
                for i in range(2):
                    if q in (R, GATE):
                        dve.wait_ge(lo_done[q - 2], 2 * s.n + i + 1)
                    elif s.least >= 1:
                        dve.wait_ge(lo_done[q + 2], 2 * s.n - 1 + i)
                    for e in range(2):
                        c = 2 * i + e
                        last = dve.scalar_tensor_tensor(raw_mix[(2 * q + i) % 4][:, e, :], dx[:, c, :],
                                                        vec[:, VEC_MV + q, c:c + 1], xnT[s.u][:, c, 0:T],
                                                        ALU.mult, ALU.add)
                    last.then_inc(raw_done[q], 1)

            def low_part(s, q):
                for i in range(2):
                    split_low(dve, s, q, i)

            def recur(s, p):
                dve.wait_ge(proj_done, 8 * s.n + 2 * K + p + 1)
                for m in (2 * p, 2 * p + 1):
                    dve.wait_ge(v_done, C * s.n + m + 1)
                    dve.scalar_tensor_tensor(kv[:, m, :], proj_ps[2 + p][:, m % 2, :], vec[:, VEC_BK, m:m + 1],
                                             vS[:, m, :], ALU.add, ALU.mult).then_inc(kv_done, 1)
                for m in (2 * p, 2 * p + 1):
                    dve.wait_ge(kv_done, C * s.n + m + 1)
                    if s.least >= 2:
                        dve.wait_ge(carried, 2 * s.n - 3 + p)
                    dve.tensor_tensor_scan(acc[:, m, :], decay[:, m:m + 1].to_broadcast([P, T]), kv[:, m, :],
                                           carry[s.u][:, m:m + 1], ALU.mult, ALU.add).then_inc(scan_done, 1)
                dve.wait_ge(scan_done, C * s.n + 2 * p + 2)
                dve.tensor_copy(carry[s.u][:, 2 * p:2 * p + 2], acc[:, 2 * p:2 * p + 2, T - 1]).then_inc(carried, 1)
                for m in (2 * p, 2 * p + 1):
                    dve.scalar_tensor_tensor(kv[:, m, :], kv[:, m, :], vec[:, VEC_U, m:m + 1],
                                             acc[:, m, :], ALU.mult, ALU.add).then_inc(wkv_done, 1)

            def receive(s, p):
                dve.wait_ge(proj_done, 8 * s.n + 2 * R + p + 1)
                if s.least >= 1:
                    dve.wait_ge(centered, 2 * s.n)
                for m in (2 * p, 2 * p + 1):
                    dve.wait_ge(wkv_done, C * s.n + m + 1)
                    dve.scalar_tensor_tensor(rw[:, m, :], proj_ps[p][:, m % 2, :], vec[:, VEC_BR, m:m + 1],
                                             kv[:, m, :], ALU.add, ALU.mult).then_inc(rw_done, 1)

            def route(f, part):
                links = [20 * part]

                def link(ins):
                    links[0] += 1
                    ins.then_inc(routed, 1)
                    dve.wait_ge(routed, GATE_LINKS * f.n + links[0])

                def best_of(i):
                    dve.wait_ge(ex_done, 2 * f.n + i + 1)
                    link(dve.tensor_scalar(den[:], ex[i][:].rearrange("p g e -> p (g e)"), 1.0, None, ALU.add))
                    link(dve.reciprocal(den[:], den[:]))
                    link(dve.tensor_scalar(pos[:], den[:], float(SEGS), None, ALU.mult))
                    link(dve.tensor_tensor(steps_ge[:], pos[:].unsqueeze(1).to_broadcast([P, KNOTS, E]),
                                           cst[:, CST_FLOOR:CST_FLOOR + KNOTS].unsqueeze(2).to_broadcast([P, KNOTS, E]),
                                           ALU.is_ge))
                    link(dve.tensor_tensor(seg[:], steps_ge[:, 0:SEGS, :], steps_ge[:, 1:KNOTS, :], ALU.subtract))
                    for w in range(3):
                        link(dve.tensor_tensor(pick[:, w, :, :], seg[:],
                                               curve[:, w, :].unsqueeze(2).to_broadcast([P, SEGS, E]), ALU.mult))
                    link(dve.tensor_reduce(piece[:], pick[:].rearrange("p w k e -> p w e k"), X, ALU.add))
                    link(dve.tensor_tensor(pos[:], pos[:], piece[:, 2, :], ALU.subtract))
                    link(dve.tensor_tensor(pos[:], pos[:], piece[:, 1, :], ALU.mult))
                    link(dve.tensor_tensor(val[:].rearrange("p g e -> p (g e)"), piece[:, 0, :], pos[:], ALU.add))
                    link(dve.tensor_reduce(best[:], val[:], X, ALU.max))
                    link(dve.tensor_tensor(is_best[:], val[:], best[:].unsqueeze(2).to_broadcast([P, G, CLUSTERS]),
                                           ALU.is_equal))
                    link(dve.scalar_tensor_tensor(cand[:], is_best[:], -float(CLUSTERS),
                                                  cst[:, CST_IOTA8:CST_IOTA8 + CLUSTERS].unsqueeze(1)
                                                  .to_broadcast([P, G, CLUSTERS]), ALU.mult, ALU.add))
                    link(dve.tensor_reduce(first[:], cand[:], X, ALU.min))
                    link(dve.tensor_tensor(hot[i][:], cst[:, CST_IOTA:CST_IOTA + CLUSTERS].unsqueeze(1)
                                           .to_broadcast([P, G, CLUSTERS]),
                                           first[:].unsqueeze(2).to_broadcast([P, G, CLUSTERS]), ALU.is_equal))

                if part == 0:
                    dve.wait_ge(scores_ps, f.n + 1)
                    dve.tensor_scalar(sc[:], turn_ps[:, 0:G * COLS].rearrange("p (g e) -> p g e", g=G),
                                      neg_it[:, 2:3], EXP_MAX, ALU.mult, ALU.min).then_inc(sc_done, 1)
                    best_of(0)
                    for g in range(G):
                        link(dve.tensor_tensor(prod[:, g, :, :], sc[:, g, 0:TILES].rearrange("p (k t) -> p t k", t=TPC),
                                               hot[0][:, g, :].unsqueeze(1).to_broadcast([P, TPC, CLUSTERS]), ALU.mult))
                    link(dve.tensor_reduce(sel[:], prod[:], X, ALU.add))
                    assert links[0] == 20
                else:
                    best_of(1)
                    for g in range(G):
                        if f.least >= 1:
                            dve.wait_ge(ohT_ps, f.n)
                        link(dve.tensor_tensor(onehot[:, g, 0, :].rearrange("p (k t) -> p k t", t=TPC),
                                               hot[0][:, g, :].unsqueeze(2).to_broadcast([P, CLUSTERS, TPC]),
                                               hot[1][:, g, :].unsqueeze(1).to_broadcast([P, CLUSTERS, TPC]), ALU.mult))
                    link(dve.tensor_copy(onehot[:, :, 1, :], onehot[:, :, 0, :]))
                    assert links[0] == GATE_LINKS

            def magnitude(f):
                links = [0]

                def link(ins):
                    links[0] += 1
                    ins.then_inc(spline, 1)
                    dve.wait_ge(spline, MAG_LINKS * f.n + links[0])

                dve.wait_ge(comp_done, f.n + 1)
                for g, bank in enumerate((turn_ps, side_ps)):
                    dve.wait_ge(tables_ps, G * f.n + g + 1)
                    link(dve.tensor_copy(tS[:, g, :], bank[:, 0:TABLE]))
                link(dve.tensor_tensor(hp[:], tS[:, :, 0:2 * GRID].rearrange("p g (i e) -> p g i e", i=2),
                                       comp[:].unsqueeze(3).to_broadcast([P, G, 2, GRID]), ALU.mult))
                link(dve.tensor_tensor(hh[:], hp[:, :, 0, :], hp[:, :, 1, :], ALU.add))
                link(dve.tensor_tensor(hh[:], hh[:], tS[:, :, 2 * GRID:3 * GRID], ALU.add))
                link(dve.scalar_tensor_tensor(hh[:], hh[:], 0.0, tS[:, :, 3 * GRID:4 * GRID], ALU.max, ALU.mult))
                link(dve.tensor_reduce(mag[:], hh[:], X, ALU.add))
                link(dve.tensor_tensor(mag[:], mag[:], tS[:, :, 4 * GRID], ALU.add))
                link(dve.tensor_scalar(mag[:], mag[:], row[:, ROW_OUTSCALE:ROW_OUTSCALE + 1], None, ALU.mult))
                assert links[0] == MAG_LINKS

            def body(s, do_mix, do_proj, do_norm, do_route, do_end):
                a, h, f, e = (s.back(k) for k in (-1, 1, 2, 3))
                if do_mix:
                    stats_input(a)
                if do_proj:
                    mix_input(s, GATE)
                if do_mix:
                    bias("a", a)
                if do_end:
                    magnitude(e)
                if do_norm:
                    for p in range(2):
                        dve.wait_ge(sq_done, 2 * h.n + p + 1)
                        dve.wait_ge(tg_done, C * h.n + 2 * p + 2)
                        t = tg[:, 2 * p:2 * p + 2, :].rearrange("p m t -> p (m t)")
                        dve.scalar_tensor_tensor(t, t, 1.0, head_ps[p][:], ALU.add, ALU.mult).then_inc(cg_done, 1)
                if do_end:
                    for g, bank in enumerate((turn_ps, side_ps)):
                        dve.wait_ge(dirs_ps, G * e.n + g + 1)
                        if e.least >= 1:
                            dve.wait_ge(fin_done, G * e.n)
                        dve.scalar_tensor_tensor(yb[:, g, :], bank[:], mag[:, g:g + 1], xf[e.u][:, g, :],
                                                 ALU.mult, ALU.add).then_inc(y_done, 1)
                    dve.wait_ge(y_done, G * e.n + G)
                    stats("d", e, lambda g: yb[:, g, :])
                if do_norm:
                    dve.wait_ge(var_done, h.n + 1)
                    dve.tensor_scalar(head_ve[:].rearrange("p g h -> p (g h)"), head_ps[0][:, 0:G * H], 4 * EPS, None,
                                      ALU.add).then_inc(head_ve_done, 1)
                if do_end:
                    bias("d", e)
                if do_proj:
                    recur(s, 0)
                if do_end:
                    for g in range(G):
                        dve.wait_ge(yn_done, G * e.n + g + 1)
                        dve.tensor_tensor(yb[:, g, :], yb[:, g, :], row[:, ROW_GAMMA:ROW_GAMMA + D],
                                          ALU.mult).then_inc(scaled, 1)
                if do_route:
                    route(f, 0)
                if do_norm:
                    dve.wait_ge(head_rs_done, h.n + 1)
                    if h.least >= 1:
                        dve.wait_ge(rs_turned, h.n)
                    dve.tensor_copy(head_hl[:, :, 0, :], head_rs[:]).then_inc(head_hi, 1)
                    dve.wait_ge(head_hi, h.n + 1)
                    dve.tensor_tensor(head_hl[:, :, 1, :], head_rs[:], head_hl[:, :, 0, :].bitcast(F32),
                                      ALU.subtract).then_inc(head_lo, 1)
                if do_proj:
                    recur(s, 1)
                if do_mix:
                    mix_input(a, V)
                if do_end:
                    dve.wait_ge(z_done, G * e.n + G)
                    stats("e", e, lambda g: yb[:, g, :])
                if do_proj:
                    receive(s, 0)
                if do_end:
                    bias("e", e)
                if do_proj:
                    receive(s, 1)
                if do_mix:
                    low_part(a, V)
                    mix_input(a, K)
                if do_norm:
                    for p in range(2):
                        dve.wait_ge(spread, 2 * h.n + p + 1)
                        dve.wait_ge(cg_done, 2 * h.n + p + 1)
                        if do_route:
                            dve.wait_ge(hidden_ps, f.n + 1)
                        if h.least >= 1:
                            dve.wait_ge(wo_done, G * h.n)
                        dve.tensor_tensor(oT[:, 2 * p:2 * p + 2, :].rearrange("p m t -> p (m t)"),
                                          tg[:, 2 * p:2 * p + 2, :].rearrange("p m t -> p (m t)"),
                                          head_ps[p][:], ALU.mult).then_inc(oT_done, 1)
                if do_mix:
                    mix_input(a, R)
                if do_route:
                    route(f, 1)
                if do_norm:
                    dve.wait_ge(wo_done, G * h.n + G)
                    stats("b", h, lambda g: head_ps[g][:])
                    bias("b", h)
                if do_mix:
                    low_part(a, R)
                if do_norm:
                    dve.wait_ge(x1_done, G * h.n + G)
                    stats("c", h, lambda g: x1[h.u][:, g, :])
                    bias("c", h)

            first_step = Step(0, 0, 0)
            stats_input(first_step)
            bias("a", first_step)
            for q in (V, K, R):
                mix_input(first_step, q)
                if q in (V, R):
                    low_part(first_step, q)
            schedule(dve, body)


def kernel(L0_attn_x, L0_attn_Wg_w, L0_attn_Wg_b, L0_attn_Wr_w, L0_attn_Wr_b, L0_attn_Wk_w, L0_attn_Wk_b,
           L0_attn_Wv_w, L0_attn_Wv_b, L0_attn_Wo_w, L0_attn_Wo_b, L0_attn_mg, L0_attn_mr, L0_attn_mk,
           L0_attn_mv, L0_attn_w, L0_attn_u, L0_ffn_signatures_raw, L0_ffn_knot_values, L0_ffn_temperature,
           L0_ffn_compress_w1, L0_ffn_compress_b1, L0_ffn_compress_w2, L0_ffn_compress_b2, L0_ffn_spline_w1,
           L0_ffn_spline_b1, L0_ffn_spline_w2, L0_ffn_spline_b2, L0_ffn_directions, L0_ffn_norm_gamma,
           L0_ffn_norm_beta, L0_ffn_output_scale):
    import concourse.bacc as bacc
    from concourse.bass_utils import run_bass_kernel_spmd

    def col(v):
        return np.asarray(v).reshape(C, P).T

    vecs = np.stack([col(v) for v in (L0_attn_mv, L0_attn_mk, L0_attn_mr, L0_attn_mg, L0_attn_Wv_b, L0_attn_Wk_b,
                                      L0_attn_Wr_b, L0_attn_Wg_b, L0_attn_w, L0_attn_u)], axis=1)
    table = np.concatenate([np.asarray(L0_ffn_spline_w1).reshape(TILES, 2 * GRID), np.asarray(L0_ffn_spline_b1),
                            np.asarray(L0_ffn_spline_w2).reshape(TILES, GRID)] + [np.asarray(L0_ffn_spline_b2)] * 2, axis=1)
    rows = np.concatenate([np.asarray(v) for v in (L0_ffn_norm_gamma, L0_ffn_norm_beta, L0_ffn_knot_values,
                                                   L0_ffn_temperature, L0_ffn_output_scale)])
    arrays = {
        "x": np.asarray(L0_attn_x),
        "w_proj": np.stack([np.asarray(w).T for w in (L0_attn_Wv_w, L0_attn_Wk_w, L0_attn_Wr_w, L0_attn_Wg_w)]),
        "w_out": np.asarray(L0_attn_Wo_w).T,
        "sig_raw": np.asarray(L0_ffn_signatures_raw).T,
        "comp_w1": np.asarray(L0_ffn_compress_w1),
        "comp_w2": np.asarray(L0_ffn_compress_w2),
        "table": np.concatenate([table] * G),
        "directions": np.concatenate([np.asarray(L0_ffn_directions)] * G),
        "vecs": vecs,
        "comp_b1": np.asarray(L0_ffn_compress_b1).reshape(HID, 1),
        "rows": np.broadcast_to(rows, (P, ROWS)),
        "bias_out": np.broadcast_to(np.asarray(L0_attn_Wo_b), (2 * HD, D)),
        "bias_comp": np.asarray(L0_ffn_compress_b2).reshape(1, 2),
        "consts": shape_constants()[0],
        "spread_rows": shape_constants()[1],
    }
    arrays = {k: np.ascontiguousarray(v) for k, v in arrays.items()}

    nc = bacc.Bacc("TRN2", target_bir_lowering=False, num_devices=1)
    ins = {k: nc.dram_tensor(k, v.shape, mybir.dt.from_np(v.dtype), kind="ExternalInput").ap()
           for k, v in arrays.items()}
    out = nc.dram_tensor("out", (B, N, D), F32, kind="ExternalOutput").ap()
    build(nc, **ins, out=out)
    r = run_bass_kernel_spmd(nc, [arrays], core_ids=[0])
    return r.results[0]["out"]
```

```python
from contextlib import ExitStack
from typing import NamedTuple

import numpy as np

import concourse.bass as bass
from concourse import mybir

P = 128
B, N, D = 2, 8192, 512
H = 16
HD = D // H
C = D // P
G = 2
T = G * P
BLOCKS = N // T
STEPS = B * BLOCKS
TILES, CLUSTERS = 64, 8
TPC = TILES // CLUSTERS
GRID = 16
HID = 128
KNOTS = 8
SEGS = KNOTS - 1
COLS = TILES + CLUSTERS
TABLE = 4 * GRID + 2
EPS = 1e-5
EXP_MAX = 88.5

F32 = mybir.dt.float32
F32R = mybir.dt.float32r
ALU = mybir.AluOpType
ACT = mybir.ActivationFunctionType
X = mybir.AxisListType.X

V, K, R, GATE = range(4)
OUT = 4
(VEC_MV, VEC_MK, VEC_MR, VEC_MG, VEC_BV, VEC_BK, VEC_BR, VEC_BG, VEC_W, VEC_U) = range(10)
ROW_GAMMA, ROW_BETA, ROW_KNOTS = 0, D, 2 * D
ROW_TEMP = ROW_KNOTS + KNOTS
ROW_OUTSCALE = ROW_TEMP + 1
ROWS = ROW_OUTSCALE + 1
CST_IDENT = 0
CST_CENTER = CST_IDENT + P
CST_HEADVAR = CST_CENTER + P
CST_FLOOR = CST_HEADVAR + C * H
CST_SEG = CST_FLOOR + KNOTS
CST_IOTA = CST_SEG + SEGS
CST_IOTA8 = CST_IOTA + CLUSTERS
CST_COLS = CST_IOTA8 + CLUSTERS

CURVE_LINKS = 15
CLUSTER_LINKS = CURVE_LINKS + G + 1
GATE_LINKS = CLUSTER_LINKS + CURVE_LINKS + G
READY = 14 + C
INPUT_SUMS = 2 * G + 1
MAG_LINKS = 6


class Step(NamedTuple):
    j: object
    u: int
    least: int

    @property
    def n(self):
        return self.j * 2 + self.u

    def back(self, k):
        u = (self.u - k) % 2
        return Step(self.j + (self.u - k - u) // 2, u, self.least - k)


def shape_constants():
    c = np.zeros((P, CST_COLS), np.float32)
    spread = np.zeros((2 * H, C * P), np.float32)
    p = np.arange(P)
    same_head = (p[:, None] // HD == p[None, :] // HD)
    c[:, CST_IDENT:CST_IDENT + P] = np.eye(P)
    c[:, CST_CENTER:CST_CENTER + P] = np.eye(P) - same_head / HD
    per = P // HD
    for m in range(C):
        c[p, CST_HEADVAR + m * H + m * per + p // HD] = 4.0 / HD
        for half in range(2):
            spread[half * H + m * per + p // HD, m * P + p] = 1.0
    c[:, CST_FLOOR:CST_FLOOR + KNOTS] = [-1.0] + list(range(1, SEGS)) + [1e30]
    c[:, CST_SEG:CST_SEG + SEGS] = np.arange(SEGS)
    c[:, CST_IOTA:CST_IOTA + CLUSTERS] = np.arange(CLUSTERS)
    c[:, CST_IOTA8:CST_IOTA8 + CLUSTERS] = np.arange(CLUSTERS) + CLUSTERS
    return c, spread


def build(nc, x, w_proj, w_out, sig_raw, comp_w1, comp_w2, table, directions, vecs, comp_b1,
          rows, bias_out, bias_comp, consts, spread_rows, out):
    ctx = ExitStack()
    with ctx:
        def sb(name, shape, dtype=F32):
            return ctx.enter_context(nc.sbuf_tensor(name, shape, dtype))

        def shared(name, rounded_name, shape):
            with nc.sbuf_tensor(name, shape, F32) as whole:
                pass
            return whole, sb(rounded_name, shape, F32R)

        def psum(name, shape):
            return ctx.enter_context(nc.psum_tensor(name, shape, F32))

        def sem(name):
            return ctx.enter_context(nc.semaphore(name))

        w_hi = [sb(f"w_hi{q}", [P, C, D], F32R) for q in range(5)]
        w_lo = [sb(f"w_lo{q}", [P, C, D], F32R) for q in range(5)]
        sigT = sb("sigT", [P, C, COLS])
        w1T = sb("w1T", [P, C, HID])
        w2 = sb("w2", [P, 2])
        tabs = sb("tabs", [P, TABLE], F32R)
        dirs = sb("dirs", [P, D], F32R)
        bo = sb("bo", [2 * HD, D], F32R)
        bo_ones = sb("bo_ones", [2 * HD, P], F32R)
        b2 = sb("b2", [1, 2 * G])
        vec = sb("vec", [P, 10, C])
        b1 = sb("b1", [P, 1])
        row = sb("row", [P, ROWS])
        cst = sb("cst", [P, CST_COLS])
        spreader = sb("spreader", [2 * H, C, P], F32R)
        ones = sb("ones", [1, P])
        mhalf = sb("mhalf", [P, G, H])
        expw = sb("expw", [P, C])
        decay = sb("decay", [P, C])
        bg_half = sb("bg_half", [P, C])
        neg_it = sb("neg_it", [P, 3])
        curve = sb("curve", [P, 3, SEGS])
        csum = sb("csum", [P, C, CLUSTERS])
        seed_st = sb("seed_st", [B, 6])
        seed_mv = sb("seed_mv", [B, 2])
        seed_ve = sb("seed_ve", [B, 1])
        seed_rs = sb("seed_rs", [B, 1])
        seed = sb("seed", [P, C, B])

        xa = [sb(f"xa{u}", [P, G, D]) for u in range(2)]
        xnT = sb("xnT", [P, C, T + 1])
        dx = sb("dx", [P, C, T])
        raw_mix = [sb(f"raw_mix{i}", [P, 2, T]) for i in range(4)]
        mix_hi = [sb(f"mix_hi{q}", [P, C, T], F32R) for q in range(4)]
        mix_lo = [sb(f"mix_lo{q}", [P, C, T], F32R) for q in range(4)]
        vS = sb("vS", [P, C, T])
        kv = sb("kv", [P, C, T])
        acc, o_lo = shared("acc", "o_lo", [P, C, T])
        carry = [sb(f"carry{u}", [P, C]) for u in range(2)]
        rw = sb("rw", [P, C, T])
        tg = sb("tg", [P, C, T])
        sq = sb("sq", [P, C, T])
        head_ve = sb("head_ve", [P, G, H])
        head_rs = sb("head_rs", [P, G, H])
        head_hl = sb("head_hl", [P, G, 2, H], F32R)
        rsT = sb("rsT", [2 * H, T], F32R)
        oT = sq
        xfT, o_hi = shared("xfT", "o_hi", [P, C, T])
        at = sq[:].rearrange("p c t -> p (c t)").rearrange("p (g d) -> p g d", g=G)
        x1 = [sb(f"x1_{u}", [P, G, D]) for u in range(2)]
        xf = sb("xf", [P, G, D])
        yb = sb("yb", [P, G, D])
        st = {k: sb(f"st_{k}", [P, G, 6]) for k in "bcde"}
        mv = {k: sb(f"mv_{k}", [P, G, 2]) for k in "bcde"}
        row_sum = sb("row_sum", [P, G])
        minus_mean = sb("minus_mean", [P, G])
        square_sum = sb("square_sum", [P, G])
        eps = sb("eps", [P, 1])
        ve = {k: sb(f"ve_{k}", [P, G]) for k in "abcde"}
        rs = {k: sb(f"rs_{k}", [P, G]) for k in "abcde"}
        nb = {k: sb(f"nb_{k}", [P, G]) for k in "abcde"}
        sc = sb("sc", [P, G, COLS])
        hS = sb("hS", [P, T])
        ex = [sb(f"ex{i}", [P, G, CLUSTERS]) for i in range(2)]
        E = G * CLUSTERS
        sel = sb("sel", [P, G, TPC])
        den = sb("den", [P, E])
        pos = sb("pos", [P, E])
        steps_ge = sb("steps_ge", [P, KNOTS, E])
        seg = sb("seg", [P, SEGS, E])
        pick = sb("pick", [P, 3, SEGS, E])
        piece = sb("piece", [P, 3, E])
        val = sb("val", [P, G, CLUSTERS])
        best = sb("best", [P, G])
        is_best = sb("is_best", [P, G, CLUSTERS])
        cand = sb("cand", [P, G, CLUSTERS])
        first = sb("first", [P, G])
        hot = [sb(f"hot{i}", [P, G, CLUSTERS]) for i in range(2)]
        prod = sb("prod", [P, G, TPC, CLUSTERS])
        onehot = sb("onehot", [P, G, 2, TILES])
        ohT = sb("ohT", [P, T], F32R)
        comp = sb("comp", [P, G, 2])
        tS = sb("tS", [P, G, TABLE])
        hp = sb("hp", [P, G, 2, GRID])
        hh = sb("hh", [P, G, GRID])
        mag = sb("mag", [P, G])

        seed_x = dx[0:B, 2:4, :].rearrange("p c t -> p (c t)")
        seed_xn = tg[0:B, 0:2, :].rearrange("p c t -> p (c t)")
        raw = kv[:, :, 0:TILES]
        q_pos = vS[:, :, 0:TILES]
        q_neg = acc[:, :, 0:TILES]
        spreader_in = tg[0:2 * H, 2:4, :].rearrange("p c t -> p (c t)")
        dirs_in = rw[:, 0:2, :].rearrange("p c t -> p (c t)")
        tabs_in = rw[:, 2, 0:TABLE]
        bo_in = dx[0:2 * HD, 0:2, :].rearrange("p c t -> p (c t)")
        w_in = [[x1[0][:], x1[1][:]], [yb[:], at], [xf[:], xfT[:].rearrange("p c t -> p (c t)").rearrange(
            "p (g d) -> p g d", g=G)], [x1[0][:], x1[1][:]], [yb[:], at]]

        proj_ps = [psum(f"proj_ps{i}", [P, 2, T]) for i in range(4)]
        turn_ps = psum("turn_ps", [P, 512])
        head_ps = [psum(f"head_ps{p}", [P, 512]) for p in range(2)]
        side_ps = psum("side_ps", [P, 512])

        weights_in = sem("weights_in")
        w_half_in = [sem(f"w_half_in{q}") for q in range(5)]
        w_hi_done = sem("w_hi_done")
        w_lo_done = sem("w_lo_done")
        xa_in = [sem(f"xa_in{u}") for u in range(2)]
        xr_in = [sem(f"xr_in{u}") for u in range(2)]
        stored = [sem(f"stored{u}") for u in range(2)]
        setup_v = sem("setup_v")
        setup_a = sem("setup_a")
        setup_p = sem("setup_p")
        setup_t = sem("setup_t")
        ready = sem("ready")
        stat = {k: sem(f"stat_{k}") for k in "bcde"}
        mean_var = {k: sem(f"mean_var_{k}") for k in "bcde"}
        input_sums = sem("input_sums")
        var_eps = {k: sem(f"var_eps_{k}") for k in "abcde"}
        rstd = {k: sem(f"rstd_{k}") for k in "abcde"}
        biased = {k: sem(f"biased_{k}") for k in "abcde"}
        xn_done = sem("xn_done")
        xn_turned = sem("xn_turned")
        xnT_done = sem("xnT_done")
        dx_done = sem("dx_done")
        raw_done = [sem(f"raw_done{q}") for q in range(4)]
        hi_done = [sem(f"hi_done{q}") for q in range(4)]
        lo_done = [sem(f"lo_done{q}") for q in range(4)]
        proj_done = sem("proj_done")
        v_done = sem("v_done")
        kv_done = sem("kv_done")
        scan_done = sem("scan_done")
        carried = sem("carried")
        wkv_done = sem("wkv_done")
        rw_done = sem("rw_done")
        tg_done = sem("tg_done")
        centered = sem("centered")
        sq_done = sem("sq_done")
        cg_done = sem("cg_done")
        var_done = sem("var_done")
        head_ve_done = sem("head_ve_done")
        head_rs_done = sem("head_rs_done")
        head_hi = sem("head_hi")
        head_lo = sem("head_lo")
        rs_turned = sem("rs_turned")
        rsT_done = sem("rsT_done")
        spread = sem("spread")
        oT_done = sem("oT_done")
        o_hi_done = sem("o_hi_done")
        o_lo_done = sem("o_lo_done")
        wo_done = sem("wo_done")
        at_done = sem("at_done")
        x1_done = sem("x1_done")
        xf_done = sem("xf_done")
        xf_turned = sem("xf_turned")
        xfT_done = sem("xfT_done")
        hidden_ps = sem("hidden_ps")
        scores_ps = sem("scores_ps")
        sc_done = sem("sc_done")
        ex_done = sem("ex_done")
        routed = sem("routed")
        hS_done = sem("hS_done")
        comp_ps = sem("comp_ps")
        comp_done = sem("comp_done")
        ohT_ps = sem("ohT_ps")
        ohT_done = sem("ohT_done")
        tables_ps = sem("tables_ps")
        tS_done = sem("tS_done")
        spline = sem("spline")
        dirs_ps = sem("dirs_ps")
        y_done = sem("y_done")
        yn_done = sem("yn_done")
        scaled = sem("scaled")
        z_done = sem("z_done")
        zn_done = sem("zn_done")
        fin_done = sem("fin_done")

        x_t = x.rearrange("s (j g p) d -> s j p g d", g=G, p=P)
        out_t = out.rearrange("s (j g p) d -> s j p g d", g=G, p=P)
        ident = cst[:, CST_IDENT:CST_IDENT + P]
        center = cst[:, CST_CENTER:CST_CENTER + P]
        N_WEIGHTS = 13

        def schedule(eng, body):
            body(Step(0, 0, 0), True, True, False, False, False)
            body(Step(0, 1, 1), True, True, True, False, False)
            body(Step(1, 0, 2), True, True, True, True, False)
            body(Step(1, 1, 3), True, True, True, True, True)
            with eng.Fori(2, BLOCKS - 1) as j:
                for u in range(2):
                    body(Step(j, u, 4 + u), True, True, True, True, True)
            j = BLOCKS - 1
            body(Step(j, 0, 2 * j), True, True, True, True, True)
            body(Step(j, 1, 2 * j + 1), False, True, True, True, True)
            body(Step(j + 1, 0, 2 * j + 2), False, False, True, True, True)
            body(Step(j + 1, 1, 2 * j + 3), False, False, False, True, True)
            body(Step(j + 2, 0, 2 * j + 4), False, False, False, False, True)

        block = ctx.enter_context(nc.Block())

        @block.sync
        def _(sp):
            for u in range(2):
                sp.dma_start(xa[u][:], x_t[u, 0]).then_inc(xa_in[u], 16)
            sp.dma_start(seed_x, x[:, N - 1, :]).then_inc(weights_in, 16)
            sp.dma_start(cst[:], consts).then_inc(weights_in, 16)
            sp.dma_start(spreader_in, spread_rows).then_inc(weights_in, 16)
            sp.dma_start(vec[:], vecs).then_inc(weights_in, 16)
            sp.dma_start(raw, sig_raw.rearrange("(c p) o -> p c o", p=P)).then_inc(weights_in, 16)
            sp.dma_start(w1T[:], comp_w1.rearrange("(c p) o -> p c o", p=P)).then_inc(weights_in, 16)
            sp.dma_start(w2[:], comp_w2).then_inc(weights_in, 16)
            sp.dma_start(tabs_in, table).then_inc(weights_in, 16)
            sp.dma_start(dirs_in, directions).then_inc(weights_in, 16)
            sp.dma_start(b1[:], comp_b1).then_inc(weights_in, 16)
            sp.dma_start(b2[:], bias_comp).then_inc(weights_in, 16)
            sp.dma_start(bo_in, bias_out).then_inc(weights_in, 16)
            sp.dma_start(row[:], rows).then_inc(weights_in, 16)
            for q in range(5):
                if q >= 3:
                    sp.wait_ge(w_lo_done, 2 * q - 4)
                halves = (w_out if q == OUT else w_proj[q]).rearrange("(i c p) o -> i p c o", i=2, p=P)
                for i in range(2):
                    sp.dma_start(w_in[q][i], halves[i]).then_inc(w_half_in[q], 16)

            def body(s, do_mix, do_proj, do_norm, do_route, do_end):
                h, e = s.back(1), s.back(3)
                if do_mix and s.least + 2 < STEPS and do_proj:
                    sp.wait_ge(xn_turned, G * s.n + G)
                    sp.nop(nofuse=True)
                    sp.dma_start(xa[s.u][:], x_t[s.u, s.j + 1]).then_inc(xa_in[s.u], 16)
                if do_end:
                    sp.wait_ge(fin_done, G * e.n + G)
                    sp.nop(nofuse=True)
                    sp.dma_start(out_t[e.u, e.j], x1[e.u][:]).then_inc(stored[e.u], 16)
                if do_norm:
                    if h.least < 2:
                        sp.wait_ge(w_lo_done, 8)
                    if h.least >= 2:
                        sp.wait_ge(stored[h.u], h.j * 16)
                        sp.nop(nofuse=True)
                    sp.dma_start(x1[h.u][:], x_t[h.u, h.j]).then_inc(xr_in[h.u], 16)

            schedule(sp, body)
            for u in range(2):
                sp.wait_ge(stored[u], 16 * BLOCKS)

        @block.gpsimd
        def _(pool):
            pool.memset(mhalf[:], -0.5).then_inc(setup_p, 1)
            pool.memset(ones[:], 1.0).then_inc(setup_p, 1)
            pool.memset(eps[:], EPS).then_inc(setup_p, 1)
            for u in range(2):
                pool.memset(carry[u][:], 0.0).then_inc(setup_p, 1)
            pool.memset(bo[:].bitcast(F32), 0.0).then_inc(setup_p, 1)
            pool.memset(bo_ones[:].bitcast(F32), 1.0).then_inc(setup_p, 1)
            pool.wait_ge(setup_p, 7)
            pool.wait_ge(setup_v, 3)
            pool.tensor_tensor(seed_rs[:], seed_ve[:], mhalf[0:B, 0, 0:1], ALU.pow).then_inc(setup_p, 1)

            def root(k, s):
                pool.wait_ge(var_eps[k], s.n + 1)
                pool.tensor_tensor(rs[k][:], ve[k][:], mhalf[:, 0, 0:G], ALU.pow).then_inc(rstd[k], 1)

            def root_input(s):
                root("a", s)
                pool.wait_ge(rstd["a"], s.n + 1)
                pool.tensor_tensor(nb["a"][:], minus_mean[:], rs["a"][:], ALU.mult).then_inc(biased["a"], 1)

            def low_heads(s):
                for p in range(2):
                    pool.wait_ge(o_hi_done, 2 * s.n + p + 1)
                    if s.least >= 1:
                        pool.wait_ge(wo_done, G * s.n)
                    cs = slice(2 * p, 2 * p + 2)
                    pool.tensor_tensor(o_lo[:, cs, :], oT[:, cs, :], o_hi[:, cs, :].bitcast(F32),
                                       ALU.subtract).then_inc(o_lo_done, 1)

            def low_part(s, q):
                for i in range(2):
                    pool.wait_ge(hi_done[q], 2 * s.n + i + 1)
                    if s.least >= 1:
                        pool.wait_ge(proj_done, 8 * s.n - 8 + 2 * q + 2)
                    cs = slice(2 * i, 2 * i + 2)
                    pool.tensor_tensor(mix_lo[q][:, cs, :], raw_mix[(2 * q + i) % 4][:],
                                       mix_hi[q][:, cs, :].bitcast(F32), ALU.subtract).then_inc(lo_done[q], 1)

            def body(s, do_mix, do_proj, do_norm, do_route, do_end):
                a, h, f, e = (s.back(k) for k in (-1, 1, 2, 3))
                if do_proj:
                    low_part(s, R)
                if do_route:
                    root("c", f)
                if do_end:
                    root("d", e)
                if do_norm:
                    pool.wait_ge(head_ve_done, h.n + 1)
                    pool.tensor_tensor(head_rs[:], head_ve[:], mhalf[:], ALU.pow).then_inc(head_rs_done, 1)
                if do_end:
                    for g in range(G):
                        pool.wait_ge(scaled, G * e.n + g + 1)
                        pool.tensor_tensor(yb[:, g, :], yb[:, g, :], row[:, ROW_BETA:ROW_BETA + D],
                                           ALU.add).then_inc(z_done, 1)
                if do_proj:
                    low_part(s, GATE)
                if do_end:
                    root("e", e)
                if do_norm:
                    if do_proj:
                        pool.wait_ge(wkv_done, C * s.n + C)
                        pool.wait_ge(carried, 2 * s.n + 2)
                    low_heads(h)
                if do_mix:
                    low_part(a, V)
                if do_end:
                    for g in range(G):
                        pool.wait_ge(zn_done, G * e.n + g + 1)
                        pool.tensor_tensor(x1[e.u][:, g, :], x1[e.u][:, g, :], yb[:, g, :],
                                           ALU.add).then_inc(fin_done, 1)
                if do_mix:
                    low_part(a, K)
                if do_norm:
                    root("b", h)
                if do_mix and s.least + 2 < STEPS:
                    root_input(s.back(-2))
                if do_norm:
                    pool.wait_ge(xr_in[h.u], h.j * 16 + 16)
                    for g in range(G):
                        pool.wait_ge(at_done, G * h.n + g + 1)
                        pool.tensor_tensor(x1[h.u][:, g, :], x1[h.u][:, g, :], at[:, g, :],
                                           ALU.add).then_inc(x1_done, 1)

            first_step = Step(0, 0, 0)
            root_input(first_step)
            for q in (V, K):
                low_part(first_step, q)
            root_input(first_step.back(-1))
            schedule(pool, body)

        @block.scalar
        def _(act):
            act.wait_ge(weights_in, 16 * N_WEIGHTS)
            act.activation(expw[:], vec[:, VEC_W, :], ACT.Exp).then_inc(setup_a, 1)
            act.wait_ge(setup_a, 1)
            act.activation(decay[:], expw[:], ACT.Exp, scale=-1.0).then_inc(setup_a, 1)
            act.wait_ge(setup_t, 1)
            act.activation(seed[:], turn_ps[:, 0:C * B].rearrange("p (c s) -> p c s", c=C),
                           ACT.Copy).then_inc(setup_a, 1)
            act.wait_ge(setup_a, 3)
            act.wait_ge(ready, READY)
            act.activation(dirs[:], dirs_in, ACT.Copy).then_inc(setup_a, 1)
            act.activation(tabs[:], tabs_in, ACT.Copy).then_inc(setup_a, 1)
            act.wait_ge(setup_p, 7)
            for p0 in (0, HD):
                act.activation(bo[p0:p0 + 1, :], bo_in[p0:p0 + 1, :], ACT.Copy).then_inc(setup_a, 1)
            act.activation(spreader[:], spreader_in.rearrange("p (c k) -> p c k", c=C), ACT.Copy).then_inc(setup_a, 1)

            def high_weights(q):
                act.wait_ge(w_half_in[q], 32)
                for i in range(2):
                    act.activation(w_hi[q][:, 2 * i:2 * i + 2, :], w_in[q][i], ACT.Copy).then_inc(w_hi_done, 1)

            def rows_by(k, s, g, dst, src, done):
                act.wait_ge(biased[k], s.n + 1)
                act.activation(dst, src, ACT.Identity, scale=rs[k][:, g:g + 1],
                               bias=nb[k][:, g:g + 1]).then_inc(done, 1)

            def stats_input(s, unused):
                act.wait_ge(xa_in[s.u], s.j * 16 + 16)
                if s.least >= 1:
                    act.wait_ge(biased["a"], s.n)
                for g in range(G):
                    act.activation(unused, xa[s.u][:, g, :], ACT.Identity,
                                   accum_out=row_sum[:, g:g + 1]).then_inc(input_sums, 1)
                    act.wait_ge(input_sums, INPUT_SUMS * s.n + g + 1)
                act.activation(minus_mean[:], row_sum[:], ACT.Copy, scale=-1.0 / D).then_inc(input_sums, 1)
                act.wait_ge(input_sums, INPUT_SUMS * s.n + G + 1)
                for g in range(G):
                    act.activation(unused, xa[s.u][:, g, :], ACT.Square, bias=minus_mean[:, g:g + 1],
                                   accum_out=square_sum[:, g:g + 1]).then_inc(input_sums, 1)
                    act.wait_ge(input_sums, INPUT_SUMS * s.n + G + g + 2)
                act.activation(ve["a"][:], square_sum[:], ACT.Identity, scale=1.0 / D,
                               bias=eps[:, 0:1]).then_inc(var_eps["a"], 1)

            def norm_input(s):
                for g in range(G):
                    rows_by("a", s, g, xa[s.u][:, g, :], xa[s.u][:, g, :], xn_done)

            def high_part(s, q):
                for i in range(2):
                    act.wait_ge(raw_done[q], 2 * s.n + i + 1)
                    if s.least >= 1:
                        act.wait_ge(proj_done, 8 * s.n - 8 + 2 * q + 2)
                        act.wait_ge(lo_done[q], 2 * s.n - 1 + i)
                    act.activation(mix_hi[q][:, 2 * i:2 * i + 2, :], raw_mix[(2 * q + i) % 4][:],
                                   ACT.Copy).then_inc(hi_done[q], 1)

            def turned_input(s):
                if s.least >= 1:
                    act.wait_ge(raw_done[GATE], 2 * s.n)
                    act.wait_ge(dx_done, s.n)
                act.activation(xnT[:, :, 0:1], seed[:, :, s.u:s.u + 1], ACT.Copy).then_inc(xnT_done, 1)
                turned = [bank[:].rearrange("p (c t) -> p c t", c=C) for bank in (turn_ps, side_ps)]
                for g in range(G):
                    act.wait_ge(xn_turned, G * s.n + g + 1)
                    act.activation(xnT[:, :, 1 + g * P:1 + g * P + P], turned[g], ACT.Copy).then_inc(xnT_done, 1)
                act.wait_ge(xnT_done, 4 * s.n + 1)
                act.activation(seed[:, :, s.u:s.u + 1], turned[G - 1][:, :, P - 1:P], ACT.Copy).then_inc(xnT_done, 1)

            def values(s, p):
                act.wait_ge(proj_done, 8 * s.n + 2 * V + p + 1)
                for i in range(2):
                    m = 2 * p + i
                    if s.least >= 1:
                        act.wait_ge(kv_done, C * s.n - C + m + 1)
                    act.activation(vS[:, m, :], proj_ps[p][:, i, :], ACT.Identity,
                                   bias=vec[:, VEC_BV, m:m + 1]).then_inc(v_done, 1)

            def gates(s, p):
                act.wait_ge(proj_done, 8 * s.n + 2 * GATE + p + 1)
                if s.least >= 1:
                    act.wait_ge(oT_done, 2 * s.n)
                for i in range(2):
                    m = 2 * p + i
                    act.activation(tg[:, m, :], proj_ps[2 + p][:, i, :], ACT.Tanh, scale=0.5,
                                   bias=bg_half[:, m:m + 1]).then_inc(tg_done, 1)

            def high_heads(s, routed_step):
                for p in range(2):
                    act.wait_ge(oT_done, 2 * s.n + p + 1)
                    if routed_step:
                        act.wait_ge(scores_ps, routed_step.n + 1)
                    if s.least >= 1:
                        act.wait_ge(wo_done, G * s.n)
                    act.activation(o_hi[:, 2 * p:2 * p + 2, :], oT[:, 2 * p:2 * p + 2, :],
                                   ACT.Copy).then_inc(o_hi_done, 1)

            def body(s, do_mix, do_proj, do_norm, do_route, do_end):
                a, h, f, e = (s.back(k) for k in (-1, 1, 2, 3))
                if do_proj:
                    values(s, 0)
                if do_route:
                    for g in range(G):
                        rows_by("b", f, g, at[:, g, :], head_ps[g][:], at_done)
                if do_end:
                    act.wait_ge(ohT_ps, e.n + 1)
                    if e.least >= 1:
                        act.wait_ge(dirs_ps, G * e.n)
                    act.activation(ohT[:], turn_ps[:, 0:T], ACT.Copy).then_inc(ohT_done, 1)
                if do_proj:
                    values(s, 1)
                if do_end:
                    for g, bank in enumerate((turn_ps, side_ps)):
                        act.wait_ge(tables_ps, G * e.n + g + 1)
                        if e.least >= 1:
                            act.wait_ge(spline, MAG_LINKS * e.n)
                        act.activation(tS[:, g, :], bank[:, 0:TABLE], ACT.Copy).then_inc(tS_done, 1)
                if do_mix:
                    norm_input(a)
                if do_proj:
                    high_part(s, GATE)
                if do_norm:
                    for p in range(2):
                        act.wait_ge(centered, 2 * h.n + p + 1)
                        if h.least >= 1:
                            act.wait_ge(x1_done, G * h.n)
                        act.activation(sq[:, 2 * p:2 * p + 2, :],
                                       head_ps[p][:].rearrange("p (m t) -> p m t", m=2),
                                       ACT.Square).then_inc(sq_done, 1)
                if do_mix:
                    turned_input(a)
                if do_route:
                    if f.least >= 1:
                        act.wait_ge(xf_turned, G * f.n)
                    if do_end:
                        act.wait_ge(y_done, G * e.n + G)
                    for g in range(G):
                        rows_by("c", f, g, xf[:, g, :], x1[f.u][:, g, :], xf_done)
                if do_route:
                    act.wait_ge(wo_done, G * f.n + G)
                    for g, bank in enumerate((turn_ps, side_ps)):
                        act.wait_ge(xf_turned, G * f.n + g + 1)
                        act.activation(xfT[:, :, g * P:g * P + P],
                                       bank[:].rearrange("p (c t) -> p c t", c=C), ACT.Copy).then_inc(xfT_done, 1)
                if do_end:
                    for g in range(G):
                        rows_by("d", e, g, yb[:, g, :], yb[:, g, :], yn_done)
                if do_mix:
                    high_part(a, V)
                if do_route:
                    act.wait_ge(hidden_ps, f.n + 1)
                    if f.least >= 1:
                        act.wait_ge(comp_ps, f.n)
                    act.activation(hS[:], side_ps[:, 0:T], ACT.Gelu, bias=b1[:, 0:1]).then_inc(hS_done, 1)
                    act.wait_ge(sc_done, f.n + 1)
                    act.activation(ex[0][:], sc[:, :, TILES:COLS], ACT.Exp).then_inc(ex_done, 1)
                if do_norm:
                    act.wait_ge(rs_turned, h.n + 1)
                    if h.least >= 1:
                        act.wait_ge(spread, 2 * h.n)
                    act.activation(rsT[:], head_ps[1][0:2 * H, 0:T], ACT.Copy).then_inc(rsT_done, 1)
                if do_mix and s.least + 2 < STEPS:
                    if do_route:
                        act.wait_ge(scores_ps, f.n + 1)
                    stats_input(s.back(-2), xfT[:, 0:2, :].rearrange("p c t -> p (c t)"))
                if do_norm:
                    high_heads(h, f if do_route else None)
                if do_route:
                    act.wait_ge(routed, GATE_LINKS * f.n + CLUSTER_LINKS)
                    act.activation(ex[1][:], sel[:], ACT.Exp).then_inc(ex_done, 1)
                if do_end:
                    for g in range(G):
                        rows_by("e", e, g, yb[:, g, :], yb[:, g, :], zn_done)
                if do_mix:
                    high_part(a, K)
                if do_route:
                    act.wait_ge(comp_ps, f.n + 1)
                    if f.least >= 1:
                        act.wait_ge(spline, MAG_LINKS * f.n)
                    act.activation(comp[:], side_ps[:, 0:2 * G].rearrange("p (g o) -> p g o", g=G),
                                   ACT.Tanh).then_inc(comp_done, 1)
                if do_proj:
                    gates(s, 0)
                if do_proj:
                    gates(s, 1)
                if do_mix:
                    high_part(a, R)

            first_step = Step(0, 0, 0)
            free = acc[:, 0:2, :].rearrange("p c t -> p (c t)")
            stats_input(first_step, free)
            norm_input(first_step)
            for q in (V, K):
                high_weights(q)
            turned_input(first_step)
            high_weights(R)
            for q in (V, K):
                high_part(first_step, q)
            for q in (GATE, OUT):
                high_weights(q)
            high_part(first_step, R)
            stats_input(first_step.back(-1), free)
            act.wait_ge(w_lo_done, 10)
            schedule(act, body)

        @block.tensor
        def _(pe):
            pe.wait_ge(weights_in, 16 * N_WEIGHTS)
            pe.wait_ge(setup_v, 4)
            for c in range(C):
                last = pe.transpose(turn_ps[:, c * B:c * B + B], seed_xn[:, c * P:c * P + P], ident[0:B, 0:B])
            last.then_inc(setup_t, 1)
            pe.wait_ge(setup_a, 3)

            def turn_input(s, g):
                pe.wait_ge(xn_done, G * s.n + g + 1)
                for c in range(C):
                    last = pe.transpose((turn_ps, side_ps)[g][:, c * P:c * P + P],
                                        xa[s.u][:, g, c * P:c * P + P], ident)
                last.then_inc(xn_turned, 1)

            def project(s, q, p):
                if s.least == 0:
                    pe.wait_ge(w_lo_done, 2 * q + 2)
                pe.wait_ge(hi_done[q], 2 * s.n + 2)
                pe.wait_ge(lo_done[q], 2 * s.n + 2)
                if q == V and s.least >= 1:
                    pe.wait_ge(rw_done, C * s.n - C + 2 * p + 2)
                if q == K and s.least >= 1:
                    pe.wait_ge(tg_done, C * s.n - C + 2 * p + 2)
                if q == R:
                    pe.wait_ge(v_done, C * s.n + 2 * p + 2)
                if q == GATE:
                    pe.wait_ge(kv_done, C * s.n + 2 * p + 2)
                bank = proj_ps[2 * (q % 2) + p]
                for i in range(2):
                    m = 2 * p + i
                    for c in range(C):
                        cols = slice(m * P, m * P + P)
                        pe.matmul(bank[:, i, :], w_hi[q][:, c, cols], mix_hi[q][:, c, :], start=(c == 0), stop=False)
                        pe.matmul(bank[:, i, :], w_hi[q][:, c, cols], mix_lo[q][:, c, :], start=False, stop=False)
                        last = pe.matmul(bank[:, i, :], w_lo[q][:, c, cols], mix_hi[q][:, c, :],
                                         start=False, stop=(c == C - 1))
                last.then_inc(proj_done, 1)

            def center_pair(s, p):
                pe.wait_ge(rw_done, C * s.n + 2 * p + 2)
                if s.least >= 1:
                    pe.wait_ge(at_done, G * s.n)
                for i in range(2):
                    last = pe.matmul(head_ps[p][:, i * T:i * T + T], center, rw[:, 2 * p + i, :],
                                     start=True, stop=True)
                last.then_inc(centered, 1)

            def body(s, do_mix, do_proj, do_norm, do_route, do_end):
                a, h, f, e = (s.back(k) for k in (-1, 1, 2, 3))
                if do_proj:
                    project(s, V, 0)
                if do_proj:
                    project(s, V, 1)
                if do_end:
                    pe.wait_ge(routed, GATE_LINKS * e.n + GATE_LINKS)
                    for g in range(G):
                        last = pe.transpose(turn_ps[:, g * P:g * P + P],
                                            onehot[:, g, :, :].rearrange("p i e -> p (i e)"), ident)
                    last.then_inc(ohT_ps, 1)
                if do_norm:
                    center_pair(h, 0)
                if do_end:
                    pe.wait_ge(comp_done, e.n + 1)
                    pe.wait_ge(ohT_done, e.n + 1)
                    for g, bank in enumerate((turn_ps, side_ps)):
                        pe.matmul(bank[:, 0:TABLE], ohT[:, g * P:g * P + P], tabs[:],
                                  start=True, stop=True).then_inc(tables_ps, 1)
                if do_norm:
                    center_pair(h, 1)
                if do_end:
                    for g, bank in enumerate((turn_ps, side_ps)):
                        pe.wait_ge(tS_done, G * e.n + 1 + g)
                        pe.matmul(bank[:], ohT[:, g * P:g * P + P], dirs[:], start=True, stop=True).then_inc(dirs_ps, 1)
                if do_proj:
                    project(s, K, 0)
                if do_mix:
                    for g in range(G):
                        if do_end:
                            pe.wait_ge(y_done, G * e.n + g + 1)
                        else:
                            pe.wait_ge(xnT_done, 4 * s.n + 4)
                        turn_input(a, g)
                if do_norm:
                    pe.wait_ge(sq_done, 2 * h.n + 2)
                    pe.wait_ge(cg_done, 2 * h.n + 1)
                    for g in range(G):
                        for m in range(C):
                            last = pe.matmul(head_ps[0][:, g * H:g * H + H], sq[:, m, g * P:g * P + P],
                                             cst[:, CST_HEADVAR + m * H:CST_HEADVAR + m * H + H],
                                             start=(m == 0), stop=(m == C - 1))
                    last.then_inc(var_done, 1)
                if do_proj:
                    project(s, K, 1)
                if do_route:
                    for g, bank in enumerate((turn_ps, side_ps)):
                        pe.wait_ge(xf_done, G * f.n + g + 1)
                        if do_mix:
                            pe.wait_ge(xnT_done, 4 * a.n + 2 + 2 * g)
                        elif do_end:
                            pe.wait_ge(y_done, G * e.n + g + 1)
                        for c in range(C):
                            last = pe.transpose(bank[:, c * P:c * P + P], xf[:, g, c * P:c * P + P], ident)
                        last.then_inc(xf_turned, 1)
                if do_proj:
                    project(s, R, 0)
                if do_route:
                    pe.wait_ge(xfT_done, G * f.n + G)
                    for c in range(C):
                        last = pe.matmul(side_ps[:, 0:T], w1T[:, c, :], xfT[:, c, :],
                                         start=(c == 0), stop=(c == C - 1))
                    last.then_inc(hidden_ps, 1)
                    for g in range(G):
                        for c in range(C):
                            last = pe.matmul(turn_ps[:, g * COLS:g * COLS + COLS], xfT[:, c, g * P:g * P + P],
                                             sigT[:, c, :], start=(c == 0), stop=(c == C - 1))
                    last.then_inc(scores_ps, 1)
                if do_norm:
                    pe.wait_ge(head_lo, h.n + 1)
                    pe.wait_ge(cg_done, 2 * h.n + 2)
                    for g in range(G):
                        last = pe.transpose(head_ps[1][0:2 * H, g * P:g * P + P],
                                            head_hl[:, g, :, :].rearrange("p i h -> p (i h)").bitcast(F32), ident)
                    last.then_inc(rs_turned, 1)
                if do_proj:
                    project(s, R, 1)
                if do_route:
                    pe.wait_ge(hS_done, f.n + 1)
                    pe.matmul(side_ps[:, 0:2 * G], ones[:], b2[:], start=True, stop=False)
                    for g in range(G):
                        last = pe.matmul(side_ps[:, 2 * g:2 * g + 2], hS[:, g * P:g * P + P], w2[:],
                                         start=False, stop=(g == G - 1))
                    last.then_inc(comp_ps, 1)
                if do_norm:
                    pe.wait_ge(rsT_done, h.n + 1)
                    for p in range(2):
                        for i in range(2):
                            m = 2 * p + i
                            last = pe.matmul(head_ps[p][:, i * T:i * T + T], spreader[:, m, :], rsT[:],
                                             start=True, stop=True)
                        last.then_inc(spread, 1)
                if do_proj:
                    project(s, GATE, 0)
                if do_proj:
                    project(s, GATE, 1)
                if do_norm:
                    if h.least == 0:
                        pe.wait_ge(w_lo_done, 10)
                    for g in range(G):
                        pe.wait_ge(oT_done, 2 * h.n + g + 1)
                        pe.matmul(head_ps[g][:], bo_ones[:], bo[:], start=True, stop=False)
                        for c in range(C):
                            pe.wait_ge(o_lo_done, 2 * h.n + c // 2 + 1)
                            rows = slice(g * P, g * P + P)
                            pe.matmul(head_ps[g][:], o_hi[:, c, rows], w_hi[OUT][:, c, :], start=False, stop=False)
                            pe.matmul(head_ps[g][:], o_hi[:, c, rows], w_lo[OUT][:, c, :], start=False, stop=False)
                            last = pe.matmul(head_ps[g][:], o_lo[:, c, rows], w_hi[OUT][:, c, :],
                                             start=False, stop=(c == C - 1))
                        last.then_inc(wo_done, 1)

            first_step = Step(0, 0, 0)
            turn_input(first_step, 0)
            turn_input(first_step, 1)
            pe.wait_ge(ready, READY + 4)
            schedule(pe, body)

        @block.vector
        def _(dve):
            dve.wait_ge(weights_in, 16 * N_WEIGHTS)
            dve.bn_stats(seed_st[:], seed_x).then_inc(setup_v, 1)
            dve.wait_ge(setup_v, 1)
            dve.bn_aggr(seed_mv[:], seed_st[:]).then_inc(setup_v, 1)
            dve.wait_ge(setup_v, 2)
            dve.tensor_scalar(seed_ve[:], seed_mv[:, 1:2], EPS, None, ALU.add).then_inc(setup_v, 1)
            dve.wait_ge(setup_p, 8)
            dve.tensor_scalar(seed_xn, seed_x, seed_mv[:, 0:1], seed_rs[:], ALU.subtract,
                              ALU.mult).then_inc(setup_v, 1)
            dve.tensor_scalar(neg_it[:, 0:1], row[:, ROW_TEMP:ROW_TEMP + 1], 1e-6, None, ALU.add).then_inc(ready, 1)
            dve.wait_ge(ready, 1)
            dve.reciprocal(neg_it[:, 1:2], neg_it[:, 0:1]).then_inc(ready, 1)
            dve.wait_ge(ready, 2)
            dve.tensor_scalar(neg_it[:, 2:3], neg_it[:, 1:2], -1.0, None, ALU.mult).then_inc(ready, 1)
            dve.tensor_scalar(bg_half[:], vec[:, VEC_BG, :], 0.5, None, ALU.mult).then_inc(ready, 1)
            dve.tensor_copy(curve[:, 0, :], row[:, ROW_KNOTS:ROW_KNOTS + SEGS]).then_inc(ready, 1)
            dve.tensor_tensor(curve[:, 1, :], row[:, ROW_KNOTS + 1:ROW_KNOTS + KNOTS],
                              row[:, ROW_KNOTS:ROW_KNOTS + SEGS], ALU.subtract).then_inc(ready, 1)
            dve.tensor_copy(curve[:, 2, :], cst[:, CST_SEG:CST_SEG + SEGS]).then_inc(ready, 1)
            dve.tensor_scalar(q_pos, raw, 0.3, None, ALU.is_gt).then_inc(ready, 1)
            dve.tensor_scalar(q_neg, raw, -0.3, None, ALU.is_lt).then_inc(ready, 1)
            dve.wait_ge(ready, 9)
            dve.tensor_tensor(q_pos, q_pos, q_neg, ALU.subtract).then_inc(ready, 1)
            dve.wait_ge(ready, 10)
            dve.tensor_tensor(q_pos, q_pos, raw, ALU.subtract).then_inc(ready, 1)
            dve.wait_ge(ready, 11)
            dve.tensor_tensor(sigT[:, :, 0:TILES], raw, q_pos, ALU.add).then_inc(ready, 1)
            dve.wait_ge(ready, 12)
            for c in range(C):
                dve.tensor_reduce(csum[:, c, :], sigT[:, c, 0:TILES].rearrange("p (k t) -> p k t", k=CLUSTERS),
                                  X, ALU.add).then_inc(ready, 1)
            dve.wait_ge(ready, 12 + C)
            dve.tensor_scalar(q_neg[:, :, 0:CLUSTERS], csum[:], 0.0, None, ALU.is_lt).then_inc(ready, 1)
            dve.wait_ge(ready, 13 + C)
            dve.scalar_tensor_tensor(sigT[:, :, TILES:COLS], csum[:], 0.0, q_neg[:, :, 0:CLUSTERS],
                                     ALU.is_gt, ALU.subtract).then_inc(ready, 1)
            dve.wait_ge(ready, READY)
            dve.wait_ge(setup_a, 8)
            above = slice(TILES, P)
            dve.tensor_tensor(dirs[above, :], dirs_in[above, :], dirs[above, :].bitcast(F32),
                              ALU.subtract).then_inc(ready, 1)
            dve.tensor_tensor(tabs[above, :], tabs_in[above, :], tabs[above, :].bitcast(F32),
                              ALU.subtract).then_inc(ready, 1)
            dve.tensor_tensor(bo[HD:HD + 1, :], bo_in[HD:HD + 1, :], bo[HD:HD + 1, :].bitcast(F32),
                              ALU.subtract).then_inc(ready, 1)
            dve.tensor_copy(carry[0][:], carry[0][:]).then_inc(ready, 1)

            def low_weights(q):
                for i in range(2):
                    dve.wait_ge(w_hi_done, 2 * q + i + 1)
                    dve.tensor_tensor(w_lo[q][:, 2 * i:2 * i + 2, :], w_in[q][i],
                                      w_hi[q][:, 2 * i:2 * i + 2, :].bitcast(F32), ALU.subtract).then_inc(w_lo_done, 1)

            def rows_stats(k, s, src):
                for g in range(G):
                    dve.bn_stats(st[k][:, g, :], src(g)).then_inc(stat[k], 1)

            def close_stats(k, s):
                for g in range(G):
                    dve.wait_ge(stat[k], G * s.n + g + 1)
                    dve.nop(nofuse=True)
                    dve.bn_aggr(mv[k][:, g, :], st[k][:, g, :]).then_inc(mean_var[k], 1)
                dve.wait_ge(mean_var[k], G * s.n + G)
                dve.tensor_scalar(ve[k][:], mv[k][:, :, 1], EPS, None, ALU.add).then_inc(var_eps[k], 1)

            def stats(k, s, src):
                rows_stats(k, s, src)
                close_stats(k, s)

            def bias(k, s):
                dve.wait_ge(rstd[k], s.n + 1)
                dve.scalar_tensor_tensor(nb[k][:], mv[k][:, :, 0], -1.0, rs[k][:], ALU.mult,
                                         ALU.mult).then_inc(biased[k], 1)

            def delta(s):
                dve.wait_ge(xnT_done, 4 * s.n + 3)
                if s.least >= 1:
                    dve.wait_ge(raw_done[GATE], 2 * s.n)
                dve.tensor_tensor(dx[:], xnT[:, :, 1:T + 1], xnT[:, :, 0:T],
                                   ALU.subtract).then_inc(dx_done, 1)

            def mix_chunk(s, q, c):
                i = c // 2
                if c == 0:
                    dve.wait_ge(dx_done, s.n + 1)
                if c % 2 == 0:
                    if q in (R, GATE):
                        dve.wait_ge(lo_done[q - 2], 2 * s.n + i + 1)
                    elif s.least >= 1:
                        dve.wait_ge(lo_done[q + 2], 2 * s.n - 1 + i)
                ins = dve.scalar_tensor_tensor(raw_mix[(2 * q + i) % 4][:, c % 2, :], dx[:, c, :],
                                               vec[:, VEC_MV + q, c:c + 1], xnT[:, c, 0:T], ALU.mult, ALU.add)
                if c % 2:
                    ins.then_inc(raw_done[q], 1)

            def mix_input(s, q):
                for c in range(C):
                    mix_chunk(s, q, c)

            def key_values(s, p):
                dve.wait_ge(proj_done, 8 * s.n + 2 * K + p + 1)
                for m in (2 * p, 2 * p + 1):
                    dve.wait_ge(v_done, C * s.n + m + 1)
                    dve.scalar_tensor_tensor(kv[:, m, :], proj_ps[2 + p][:, m % 2, :], vec[:, VEC_BK, m:m + 1],
                                             vS[:, m, :], ALU.add, ALU.mult).then_inc(kv_done, 1)

            def recur(s, p):
                if s.least >= 2:
                    dve.wait_ge(wo_done, G * s.n - G)
                for m in (2 * p, 2 * p + 1):
                    dve.wait_ge(kv_done, C * s.n + m + 1)
                    if s.least >= 2:
                        dve.wait_ge(carried, 2 * s.n - 3 + p)
                    dve.tensor_tensor_scan(acc[:, m, :], decay[:, m:m + 1].to_broadcast([P, T]), kv[:, m, :],
                                           carry[s.u][:, m:m + 1], ALU.mult, ALU.add).then_inc(scan_done, 1)
                for m in (2 * p, 2 * p + 1):
                    dve.wait_ge(scan_done, C * s.n + m + 1)
                    dve.scalar_tensor_tensor(kv[:, m, :], kv[:, m, :], vec[:, VEC_U, m:m + 1],
                                             acc[:, m, :], ALU.mult, ALU.add).then_inc(wkv_done, 1)
                dve.tensor_copy(carry[s.u][:, 2 * p:2 * p + 2], acc[:, 2 * p:2 * p + 2, T - 1]).then_inc(carried, 1)

            def normalise(s, p):
                dve.wait_ge(spread, 2 * s.n + p + 1)
                dve.wait_ge(cg_done, 2 * s.n + p + 1)
                dve.tensor_tensor(oT[:, 2 * p:2 * p + 2, :].rearrange("p m t -> p (m t)"),
                                  tg[:, 2 * p:2 * p + 2, :].rearrange("p m t -> p (m t)"),
                                  head_ps[p][:], ALU.mult).then_inc(oT_done, 1)

            def receive(s, m):
                if m % 2 == 0:
                    dve.wait_ge(proj_done, 8 * s.n + 2 * R + m // 2 + 1)
                    if s.least >= 1:
                        dve.wait_ge(centered, 2 * s.n)
                dve.wait_ge(wkv_done, C * s.n + m + 1)
                dve.scalar_tensor_tensor(rw[:, m, :], proj_ps[m // 2][:, m % 2, :], vec[:, VEC_BR, m:m + 1],
                                         kv[:, m, :], ALU.add, ALU.mult).then_inc(rw_done, 1)

            def linked(f, link):
                if f.least >= 1 or link:
                    dve.wait_ge(routed, GATE_LINKS * f.n + link)

            def curve_link(f, i, k):
                if k == 0:
                    dve.wait_ge(ex_done, 2 * f.n + i + 1)
                linked(f, CLUSTER_LINKS * i + k)
                if k == 0:
                    ins = dve.tensor_scalar(den[:], ex[i][:].rearrange("p g e -> p (g e)"), 1.0, None, ALU.add)
                elif k == 1:
                    ins = dve.reciprocal(den[:], den[:])
                elif k == 2:
                    ins = dve.tensor_scalar(pos[:], den[:], float(SEGS), None, ALU.mult)
                elif k == 3:
                    ins = dve.tensor_tensor(steps_ge[:], pos[:].unsqueeze(1).to_broadcast([P, KNOTS, E]),
                                            cst[:, CST_FLOOR:CST_FLOOR + KNOTS].unsqueeze(2)
                                            .to_broadcast([P, KNOTS, E]), ALU.is_ge)
                elif k == 4:
                    ins = dve.tensor_tensor(seg[:], steps_ge[:, 0:SEGS, :], steps_ge[:, 1:KNOTS, :], ALU.subtract)
                elif k == 5:
                    ins = dve.tensor_tensor(pick[:], seg[:].unsqueeze(1).to_broadcast([P, 3, SEGS, E]),
                                            curve[:].unsqueeze(3).to_broadcast([P, 3, SEGS, E]), ALU.mult)
                elif k == 6:
                    ins = dve.tensor_reduce(piece[:], pick[:].rearrange("p w k e -> p w e k"), X, ALU.add)
                elif k == 7:
                    ins = dve.tensor_tensor(pos[:], pos[:], piece[:, 2, :], ALU.subtract)
                elif k == 8:
                    ins = dve.tensor_tensor(pos[:], pos[:], piece[:, 1, :], ALU.mult)
                elif k == 9:
                    ins = dve.tensor_tensor(val[:].rearrange("p g e -> p (g e)"), piece[:, 0, :], pos[:], ALU.add)
                elif k == 10:
                    ins = dve.tensor_reduce(best[:], val[:], X, ALU.max)
                elif k == 11:
                    ins = dve.tensor_tensor(is_best[:], val[:], best[:].unsqueeze(2).to_broadcast([P, G, CLUSTERS]),
                                            ALU.is_equal)
                elif k == 12:
                    ins = dve.scalar_tensor_tensor(cand[:], is_best[:], -float(CLUSTERS),
                                                   cst[:, CST_IOTA8:CST_IOTA8 + CLUSTERS].unsqueeze(1)
                                                   .to_broadcast([P, G, CLUSTERS]), ALU.mult, ALU.add)
                elif k == 13:
                    ins = dve.tensor_reduce(first[:], cand[:], X, ALU.min)
                else:
                    ins = dve.tensor_tensor(hot[i][:], cst[:, CST_IOTA:CST_IOTA + CLUSTERS].unsqueeze(1)
                                            .to_broadcast([P, G, CLUSTERS]),
                                            first[:].unsqueeze(2).to_broadcast([P, G, CLUSTERS]), ALU.is_equal)
                ins.then_inc(routed, 1)

            def scores(f):
                dve.wait_ge(scores_ps, f.n + 1)
                dve.tensor_scalar(sc[:], turn_ps[:, 0:G * COLS].rearrange("p (g e) -> p g e", g=G),
                                  neg_it[:, 2:3], EXP_MAX, ALU.mult, ALU.min).then_inc(sc_done, 1)

            def tile_scores(f):
                linked(f, CURVE_LINKS)
                dve.wait_ge(sc_done, f.n + 1)
                for g in range(G):
                    dve.tensor_tensor(prod[:, g, :, :], sc[:, g, 0:TILES].rearrange("p (k t) -> p t k", t=TPC),
                                      hot[0][:, g, :].unsqueeze(1).to_broadcast([P, TPC, CLUSTERS]),
                                      ALU.mult).then_inc(routed, 1)
                linked(f, CURVE_LINKS + G)
                dve.tensor_reduce(sel[:], prod[:], X, ALU.add).then_inc(routed, 1)

            def chosen(f):
                linked(f, GATE_LINKS - G)
                if f.least >= 1:
                    dve.wait_ge(ohT_ps, f.n)
                for g in range(G):
                    dve.tensor_tensor(onehot[:, g, :, :].rearrange("p i (k t) -> p i k t", t=TPC),
                                      hot[0][:, g, :].unsqueeze(1).unsqueeze(3).to_broadcast([P, 2, CLUSTERS, TPC]),
                                      hot[1][:, g, :].unsqueeze(1).unsqueeze(2).to_broadcast([P, 2, CLUSTERS, TPC]),
                                      ALU.mult).then_inc(routed, 1)

            def magnitude(f):
                links = [0]

                def link(ins):
                    links[0] += 1
                    ins.then_inc(spline, 1)
                    dve.wait_ge(spline, MAG_LINKS * f.n + links[0])

                dve.wait_ge(comp_done, f.n + 1)
                dve.wait_ge(tS_done, G * f.n + G)
                link(dve.tensor_tensor(hp[:], tS[:, :, 0:2 * GRID].rearrange("p g (i e) -> p g i e", i=2),
                                       comp[:].unsqueeze(3).to_broadcast([P, G, 2, GRID]), ALU.mult))
                link(dve.tensor_tensor(hh[:], hp[:, :, 0, :], hp[:, :, 1, :], ALU.add))
                link(dve.tensor_tensor(hh[:], hh[:], tS[:, :, 2 * GRID:3 * GRID], ALU.add))
                link(dve.scalar_tensor_tensor(hh[:], hh[:], 0.0, tS[:, :, 3 * GRID:4 * GRID], ALU.max, ALU.mult))
                link(dve.tensor_reduce(mag[:], hh[:], X, ALU.add))
                for g in range(G):
                    ins = dve.tensor_scalar(mag[:, g:g + 1], mag[:, g:g + 1], tS[:, g, 4 * GRID:4 * GRID + 1],
                                            row[:, ROW_OUTSCALE:ROW_OUTSCALE + 1], ALU.add, ALU.mult)
                link(ins)
                assert links[0] == MAG_LINKS

            def body(s, do_mix, do_proj, do_norm, do_route, do_end):
                a, h, f, e = (s.back(k) for k in (-1, 1, 2, 3))
                if do_proj:
                    mix_input(s, GATE)
                if do_end:
                    magnitude(e)
                if do_end:
                    dve.wait_ge(spline, MAG_LINKS * e.n + MAG_LINKS)
                    for g, bank in enumerate((turn_ps, side_ps)):
                        dve.wait_ge(dirs_ps, G * e.n + g + 1)
                        if e.least >= 1:
                            dve.wait_ge(fin_done, G * e.n)
                        dve.scalar_tensor_tensor(yb[:, g, :], bank[:], mag[:, g:g + 1], xf[:, g, :],
                                                 ALU.mult, ALU.add).then_inc(y_done, 1)
                if do_norm:
                    for p in range(2):
                        dve.wait_ge(sq_done, 2 * h.n + p + 1)
                        dve.wait_ge(tg_done, C * h.n + 2 * p + 2)
                        t = tg[:, 2 * p:2 * p + 2, :].rearrange("p m t -> p (m t)")
                        dve.scalar_tensor_tensor(t, t, 1.0, head_ps[p][:], ALU.add, ALU.mult).then_inc(cg_done, 1)
                if do_route:
                    dve.wait_ge(x1_done, G * f.n + G)
                    stats("c", f, lambda g: x1[f.u][:, g, :])
                if do_end:
                    dve.wait_ge(y_done, G * e.n + G)
                    rows_stats("d", e, lambda g: yb[:, g, :])
                if do_route:
                    bias("c", f)
                if do_end:
                    close_stats("d", e)
                if do_norm:
                    dve.wait_ge(var_done, h.n + 1)
                    dve.tensor_scalar(head_ve[:].rearrange("p g h -> p (g h)"), head_ps[0][:, 0:G * H], 4 * EPS, None,
                                      ALU.add).then_inc(head_ve_done, 1)
                if do_mix:
                    delta(a)
                if do_proj:
                    key_values(s, 0)
                if do_end:
                    bias("d", e)
                if do_proj:
                    recur(s, 0)
                if do_mix:
                    mix_input(a, V)
                if do_end:
                    for g in range(G):
                        dve.wait_ge(yn_done, G * e.n + g + 1)
                        dve.tensor_tensor(yb[:, g, :], yb[:, g, :], row[:, ROW_GAMMA:ROW_GAMMA + D],
                                          ALU.mult).then_inc(scaled, 1)
                if do_norm:
                    dve.wait_ge(head_rs_done, h.n + 1)
                    if h.least >= 1:
                        dve.wait_ge(rs_turned, h.n)
                    dve.tensor_copy(head_hl[:, :, 0, :], head_rs[:]).then_inc(head_hi, 1)
                    dve.wait_ge(head_hi, h.n + 1)
                    dve.tensor_tensor(head_hl[:, :, 1, :], head_rs[:], head_hl[:, :, 0, :].bitcast(F32),
                                      ALU.subtract).then_inc(head_lo, 1)
                if do_proj:
                    key_values(s, 1)
                    recur(s, 1)
                if do_route:
                    scores(f)
                for k in range(CURVE_LINKS):
                    if do_mix and k in (3, 4, 5, 9):
                        mix_chunk(a, K, (3, 4, 5, 9).index(k))
                    if do_end and k == 0:
                        dve.wait_ge(z_done, G * e.n + G)
                        rows_stats("e", e, lambda g: yb[:, g, :])
                    if do_end and k == 1:
                        close_stats("e", e)
                    if do_norm and k in (6, 8):
                        normalise(h, (k - 6) // 2)
                    if do_end and k == 10:
                        bias("e", e)
                    if do_route:
                        curve_link(f, 0, k)
                if do_route:
                    tile_scores(f)
                if do_proj:
                    receive(s, 0)
                for k in range(CURVE_LINKS):
                    if do_proj and k in (0, 3, 7):
                        receive(s, {0: 1, 3: 2, 7: 3}[k])
                    if do_mix and k in (1, 4, 6, 9):
                        mix_chunk(a, R, (1, 4, 6, 9).index(k))
                    if do_norm and k == 10:
                        dve.wait_ge(wo_done, G * h.n + G)
                        rows_stats("b", h, lambda g: head_ps[g][:])
                    if do_norm and k == 11:
                        close_stats("b", h)
                    if do_route:
                        curve_link(f, 1, k)
                if do_norm:
                    bias("b", h)
                if do_route:
                    chosen(f)

            first_step = Step(0, 0, 0)
            dve.wait_ge(ready, READY + 3)
            for q in (V, K):
                low_weights(q)
            delta(first_step)
            for q in (V, K):
                mix_input(first_step, q)
            for q in (R, GATE, OUT):
                low_weights(q)
            mix_input(first_step, R)
            schedule(dve, body)


def kernel(L0_attn_x, L0_attn_Wg_w, L0_attn_Wg_b, L0_attn_Wr_w, L0_attn_Wr_b, L0_attn_Wk_w, L0_attn_Wk_b,
           L0_attn_Wv_w, L0_attn_Wv_b, L0_attn_Wo_w, L0_attn_Wo_b, L0_attn_mg, L0_attn_mr, L0_attn_mk,
           L0_attn_mv, L0_attn_w, L0_attn_u, L0_ffn_signatures_raw, L0_ffn_knot_values, L0_ffn_temperature,
           L0_ffn_compress_w1, L0_ffn_compress_b1, L0_ffn_compress_w2, L0_ffn_compress_b2, L0_ffn_spline_w1,
           L0_ffn_spline_b1, L0_ffn_spline_w2, L0_ffn_spline_b2, L0_ffn_directions, L0_ffn_norm_gamma,
           L0_ffn_norm_beta, L0_ffn_output_scale):
    import concourse.bacc as bacc
    from concourse.bass_utils import run_bass_kernel_spmd

    def col(v):
        return np.asarray(v).reshape(C, P).T

    vecs = np.stack([col(v) for v in (L0_attn_mv, L0_attn_mk, L0_attn_mr, L0_attn_mg, L0_attn_Wv_b, L0_attn_Wk_b,
                                      L0_attn_Wr_b, L0_attn_Wg_b, L0_attn_w, L0_attn_u)], axis=1)
    table = np.concatenate([np.asarray(L0_ffn_spline_w1).reshape(TILES, 2 * GRID), np.asarray(L0_ffn_spline_b1),
                            np.asarray(L0_ffn_spline_w2).reshape(TILES, GRID)] + [np.asarray(L0_ffn_spline_b2)] * 2, axis=1)
    rows = np.concatenate([np.asarray(v) for v in (L0_ffn_norm_gamma, L0_ffn_norm_beta, L0_ffn_knot_values,
                                                   L0_ffn_temperature, L0_ffn_output_scale)])
    arrays = {
        "x": np.asarray(L0_attn_x),
        "w_proj": np.stack([np.asarray(w).T for w in (L0_attn_Wv_w, L0_attn_Wk_w, L0_attn_Wr_w, L0_attn_Wg_w)]),
        "w_out": np.asarray(L0_attn_Wo_w).T,
        "sig_raw": np.asarray(L0_ffn_signatures_raw).T,
        "comp_w1": np.asarray(L0_ffn_compress_w1),
        "comp_w2": np.asarray(L0_ffn_compress_w2),
        "table": np.concatenate([table] * G),
        "directions": np.concatenate([np.asarray(L0_ffn_directions)] * G),
        "vecs": vecs,
        "comp_b1": np.asarray(L0_ffn_compress_b1).reshape(HID, 1),
        "rows": np.broadcast_to(rows, (P, ROWS)),
        "bias_out": np.broadcast_to(np.asarray(L0_attn_Wo_b), (2 * HD, D)),
        "bias_comp": np.concatenate([np.asarray(L0_ffn_compress_b2)] * G).reshape(1, 2 * G),
        "consts": shape_constants()[0],
        "spread_rows": shape_constants()[1],
    }
    arrays = {k: np.ascontiguousarray(v) for k, v in arrays.items()}

    nc = bacc.Bacc("TRN2", target_bir_lowering=False, num_devices=1)
    ins = {k: nc.dram_tensor(k, v.shape, mybir.dt.from_np(v.dtype), kind="ExternalInput").ap()
           for k, v in arrays.items()}
    out = nc.dram_tensor("out", (B, N, D), F32, kind="ExternalOutput").ap()
    build(nc, **ins, out=out)
    r = run_bass_kernel_spmd(nc, [arrays], core_ids=[0])
    return r.results[0]["out"]
```
